# Optimizing a Trainium2 kernel written in Bass

```python
import numpy as np
import jax
import jax.numpy as jnp

def _softmax(x, axis=-1):
    return jax.nn.softmax(x, axis=axis)

def _gelu(x):
    return jax.nn.gelu(x, approximate=True)

def _silu(x):
    return jax.nn.silu(x)

def _sigmoid(x):
    return jax.nn.sigmoid(x)

def _layernorm(x, axis=-1, eps=1e-05):
    m = jnp.mean(x, axis=axis, keepdims=True)
    v = jnp.var(x, axis=axis, keepdims=True)
    return (x - m) / jnp.sqrt(v + eps)

def _scatter_add(tgt, idx, src, axis=0):
    return tgt.at[idx].add(src)

def _segment_sum(src, seg, n):
    return jax.ops.segment_sum(src, seg, n)
kernel_name = 'mk_adj_preln_d2_adj_r2_8d61be'

def setup_inputs(seed: int=0):
    np.random.seed(seed)
    _w = jnp.asarray

    def _rec_inputs():
        import jax
        import jax.numpy as jnp
        _gk = jax.random.key(seed)
        x = -0.0005207 + 1.001 * jax.random.normal(jax.random.fold_in(_gk, 1), (4096, 128), jnp.float32)
        _a = jax.random.bernoulli(jax.random.fold_in(_gk, 2), 0.00390625, (4096, 4096))
        _a = jnp.logical_or(_a, jnp.swapaxes(_a, -1, -2))
        _a = jnp.logical_or(_a, jnp.eye(4096, dtype=bool))
        _af = _a.astype(jnp.float32)
        adj = _af
        return (x, adj)
    x, adj = _rec_inputs()

    def _L0_gnn_setup():
        import jax, jax.numpy as jnp
        import numpy as np
        N = 4096
        IN_F = 128
        OUT_F = 128
        ALPHA = 0.2
        key = jax.random.key(seed)
        k_x, k_adj, k_w, k_as, k_ad = jax.random.split(key, 5)
        x = jax.random.normal(k_x, (N, IN_F), dtype=jnp.float32)
        adj = (jax.random.uniform(k_adj, (N, N)) < 0.01).astype(jnp.float32)
        lim_w = float(np.sqrt(6.0 / (IN_F + OUT_F)))
        W = jax.random.uniform(k_w, (OUT_F, IN_F), minval=-lim_w, maxval=lim_w, dtype=jnp.float32)
        lim_a = float(np.sqrt(6.0 / (1 + OUT_F)))
        attn_src = jax.random.uniform(k_as, (1, OUT_F), minval=-lim_a, maxval=lim_a, dtype=jnp.float32)
        attn_dst = jax.random.uniform(k_ad, (1, OUT_F), minval=-lim_a, maxval=lim_a, dtype=jnp.float32)
        return {'x': x, 'adj': adj, 'W': W, 'attn_src': attn_src, 'attn_dst': attn_dst}
    _L0_gnn_all = _L0_gnn_setup()
    _L0_gnn_in = {k: v for k, v in _L0_gnn_all.items() if k in ('W', 'attn_src', 'attn_dst')}
    del _L0_gnn_all

    def _L1_gnn_setup():
        import jax, jax.numpy as jnp
        import numpy as np
        N, H, HEADS = (2048, 128, 3)
        ALPHA = 0.2
        NEG_INF = -9000000000000000.0

        def _sign_adj(key, n, density):
            k1, k2 = jax.random.split(key)
            mask = jax.random.uniform(k1, (n, n)) < density
            sign = jnp.where(jax.random.uniform(k2, (n, n)) < 0.5, -1.0, 1.0)
            adj = jnp.where(mask, sign, 0.0).astype(jnp.float32)
            idx = jnp.arange(n)
            return adj.at[idx, idx].set(1.0)

        def _gru_cell(x, hstate, Wih, Whh, bih, bhh):
            gi = x @ Wih.T + bih
            gh = hstate @ Whh.T + bhh
            ir, iz, inn = jnp.split(gi, 3, axis=1)
            hr, hz, hn = jnp.split(gh, 3, axis=1)
            r = jax.nn.sigmoid(ir + hr)
            z = jax.nn.sigmoid(iz + hz)
            n = jnp.tanh(inn + r * hn)
            return (1.0 - z) * n + z * hstate

        def _gat_head(h, node_adj, edge_adj, W, a):
            hW = h @ W
            hp = (node_adj > 0).astype(hW.dtype) @ hW
            hm = (node_adj < 0).astype(hW.dtype) @ hW
            e_plus = jax.nn.leaky_relu(jnp.concatenate([hp, hm], axis=1) @ a, ALPHA)[:, 0]
            e_minus = jax.nn.leaky_relu(jnp.concatenate([hm, hp], axis=1) @ a, ALPHA)[:, 0]
            att = jnp.where(edge_adj > 0, e_plus[None, :], NEG_INF)
            att = jnp.where(edge_adj < 0, e_minus[None, :], att)
            att = jax.nn.softmax(att, axis=1)
            return att * edge_adj @ hW
        key = jax.random.key(seed)
        ks = jax.random.split(key, 16)
        std = 0.01
        gain = 1.414
        return {'h': jax.random.normal(ks[0], (N, H), jnp.float32), 'node_adj': _sign_adj(ks[1], N, 0.005), 'edge_adj': _sign_adj(ks[2], N, 0.005), 'gat_W': jax.random.normal(ks[3], (HEADS, H, H), jnp.float32) * (gain / np.sqrt(H, dtype=np.float32)), 'gat_a': jax.random.normal(ks[4], (HEADS, 2 * H, 1), jnp.float32) * 0.1, 'edge_Wih': jax.random.normal(ks[5], (3 * H, H), jnp.float32) * std, 'edge_Whh': jax.random.normal(ks[6], (3 * H, H), jnp.float32) * std, 'edge_bih': jnp.zeros((3 * H,), jnp.float32), 'edge_bhh': jnp.zeros((3 * H,), jnp.float32), 'node_Wih': jax.random.normal(ks[7], (3 * H, H), jnp.float32) * std, 'node_Whh': jax.random.normal(ks[8], (3 * H, H), jnp.float32) * std, 'node_bih': jnp.zeros((3 * H,), jnp.float32), 'node_bhh': jnp.zeros((3 * H,), jnp.float32)}
    _L1_gnn_all = _L1_gnn_setup()
    _L1_gnn_in = {k: v for k, v in _L1_gnn_all.items() if k in ('gat_W', 'gat_a', 'edge_Wih', 'edge_Whh', 'edge_bih', 'edge_bhh', 'node_Wih', 'node_Whh', 'node_bih', 'node_bhh')}
    del _L1_gnn_all
    return {'x': x, 'adj': adj, 'L0_gnn_W': _L0_gnn_in['W'], 'L0_gnn_attn_src': _L0_gnn_in['attn_src'], 'L0_gnn_attn_dst': _L0_gnn_in['attn_dst'], 'L1_gnn_gat_W': _L1_gnn_in['gat_W'], 'L1_gnn_gat_a': _L1_gnn_in['gat_a'], 'L1_gnn_edge_Wih': _L1_gnn_in['edge_Wih'], 'L1_gnn_edge_Whh': _L1_gnn_in['edge_Whh'], 'L1_gnn_edge_bih': _L1_gnn_in['edge_bih'], 'L1_gnn_edge_bhh': _L1_gnn_in['edge_bhh'], 'L1_gnn_node_Wih': _L1_gnn_in['node_Wih'], 'L1_gnn_node_Whh': _L1_gnn_in['node_Whh'], 'L1_gnn_node_bih': _L1_gnn_in['node_bih'], 'L1_gnn_node_bhh': _L1_gnn_in['node_bhh']}

def reference(x, adj, L0_gnn_W, L0_gnn_attn_src, L0_gnn_attn_dst, L1_gnn_gat_W, L1_gnn_gat_a, L1_gnn_edge_Wih, L1_gnn_edge_Whh, L1_gnn_edge_bih, L1_gnn_edge_bhh, L1_gnn_node_Wih, L1_gnn_node_Whh, L1_gnn_node_bih, L1_gnn_node_bhh):
    import jax
    import jax.numpy as jnp

    def _L0_gnn_ref(x, adj, W, attn_src, attn_dst):
        import jax, jax.numpy as jnp
        import numpy as np
        N = 4096
        IN_F = 128
        OUT_F = 128
        ALPHA = 0.2
        h = x @ W.T
        a_src = (h * attn_src).sum(axis=-1)
        a_dst = (h * attn_dst).sum(axis=-1)
        scores = a_src[None, :] + a_dst[:, None]
        mask = (adj > 0).astype(h.dtype)
        s = jnp.where(scores > 0, scores, ALPHA * scores) * mask
        s = s - jnp.max(s, axis=1, keepdims=True)
        e = jnp.exp(s) * mask
        w = e / (jnp.sum(e, axis=1, keepdims=True) + 1e-08)
        out = w @ h
        return jax.nn.elu(out)

    def _L1_gnn_ref(h, node_adj, edge_adj, gat_W, gat_a, edge_Wih, edge_Whh, edge_bih, edge_bhh, node_Wih, node_Whh, node_bih, node_bhh):
        import jax, jax.numpy as jnp
        import numpy as np
        N, H, HEADS = (2048, 128, 3)
        ALPHA = 0.2
        NEG_INF = -9000000000000000.0

        def _sign_adj(key, n, density):
            k1, k2 = jax.random.split(key)
            mask = jax.random.uniform(k1, (n, n)) < density
            sign = jnp.where(jax.random.uniform(k2, (n, n)) < 0.5, -1.0, 1.0)
            adj = jnp.where(mask, sign, 0.0).astype(jnp.float32)
            idx = jnp.arange(n)
            return adj.at[idx, idx].set(1.0)

        def _gru_cell(x, hstate, Wih, Whh, bih, bhh):
            gi = x @ Wih.T + bih
            gh = hstate @ Whh.T + bhh
            ir, iz, inn = jnp.split(gi, 3, axis=1)
            hr, hz, hn = jnp.split(gh, 3, axis=1)
            r = jax.nn.sigmoid(ir + hr)
            z = jax.nn.sigmoid(iz + hz)
            n = jnp.tanh(inn + r * hn)
            return (1.0 - z) * n + z * hstate

        def _gat_head(h, node_adj, edge_adj, W, a):
            hW = h @ W
            hp = (node_adj > 0).astype(hW.dtype) @ hW
            hm = (node_adj < 0).astype(hW.dtype) @ hW
            e_plus = jax.nn.leaky_relu(jnp.concatenate([hp, hm], axis=1) @ a, ALPHA)[:, 0]
            e_minus = jax.nn.leaky_relu(jnp.concatenate([hm, hp], axis=1) @ a, ALPHA)[:, 0]
            att = jnp.where(edge_adj > 0, e_plus[None, :], NEG_INF)
            att = jnp.where(edge_adj < 0, e_minus[None, :], att)
            att = jax.nn.softmax(att, axis=1)
            return att * edge_adj @ hW
        dn = jnp.diag(node_adj)
        de = jnp.diag(edge_adj)
        idx = jnp.arange(node_adj.shape[0])
        node_adj_norm = node_adj.at[idx, idx].add(-dn)
        edge_adj_norm = edge_adj.at[idx, idx].add(-de)
        node_support = node_adj_norm @ h
        edge_output = _gru_cell(node_support, h, edge_Wih, edge_Whh, edge_bih, edge_bhh)
        edge_support = _gat_head(h, node_adj_norm, edge_adj_norm, gat_W[0], gat_a[0])
        for i in range(1, HEADS):
            edge_support = edge_support + _gat_head(h, node_adj_norm, edge_adj_norm, gat_W[i], gat_a[i])
        edge_support = edge_support / HEADS
        node_output = _gru_cell(edge_support, h, node_Wih, node_Whh, node_bih, node_bhh)
        return de[:, None] * edge_output + dn[:, None] * node_output
    h = jnp.maximum(_layernorm(x, axis=-1), 0.0)
    x = x + _L0_gnn_ref(h, adj, L0_gnn_W, L0_gnn_attn_src, L0_gnn_attn_dst)
    h = jnp.maximum(_layernorm(x, axis=-1), 0.0)
    x = x + _L1_gnn_ref(h, adj, adj, L1_gnn_gat_W, L1_gnn_gat_a, L1_gnn_edge_Wih, L1_gnn_edge_Whh, L1_gnn_edge_bih, L1_gnn_edge_bhh, L1_gnn_node_Wih, L1_gnn_node_Whh, L1_gnn_node_bih, L1_gnn_node_bhh)
    return x

_drawn_inputs = setup_inputs


def setup_inputs(seed=0):
    import zlib

    import numpy as np

    out = dict(_drawn_inputs(seed))
    spreads = {'L1_gnn_edge_bih': (0.0, 0.343),
     'L1_gnn_edge_bhh': (0.0, 0.468),
     'L1_gnn_node_bih': (0.0, 0.289),
     'L1_gnn_node_bhh': (0.0, 0.429)}
    factors = {'L1_gnn_gat_W': 3.273,
     'L1_gnn_gat_a': 6.526,
     'L1_gnn_edge_Whh': 4.352,
     'L1_gnn_node_Wih': 3.5,
     'L1_gnn_node_Whh': 4.129}
    for name, (base, spread) in spreads.items():
        noise = np.random.default_rng([zlib.crc32(name.encode()), seed]).standard_normal(out[name].shape)
        drawn = base * np.exp(spread * noise) if base else spread * noise
        out[name] = jnp.asarray(drawn.astype(out[name].dtype))
    for name, factor in factors.items():
        out[name] = (out[name] * factor).astype(out[name].dtype)
    return out
```

```python
import concourse.bass as bass
from concourse import mybir
from contextlib import ExitStack

F32, F16, BF16 = mybir.dt.float32, mybir.dt.float16, mybir.dt.bfloat16
I16, I32, U8 = mybir.dt.int16, mybir.dt.int32, mybir.dt.uint8
ALU = mybir.AluOpType
ACT = mybir.ActivationFunctionType
AX = mybir.AxisListType
ds = bass.ds


class Steps:

    def __init__(self, eng, sem, base=0):
        self.eng, self.sem, self.base, self.n = eng, sem, base, 0

    def __call__(self, instruction):
        self.n += 1
        instruction.then_inc(self.sem, 1)
        self.eng.wait_ge(self.sem, self.base + self.n)


def graph_layers(nc, x, adj_t, w0, w0_t, att_src, att_dst, gat_w, gat_w_t, gat_a,
                 e_wih_t, e_whh_t, e_bih, e_bhh, n_wih_t, n_whh_t, n_bih, n_bhh, out):
    P = 128
    N, F = x.shape
    T = N // P
    H = gat_w.shape[0]
    Q = 4
    NG = T // Q
    CW = Q * P
    C = N // CW
    F1 = F + 1
    SPLIT = 2048.0
    LOG2E = 1.4426950408889634
    LN2_HI = 0.693359375
    LN2_LO = -2.12194440e-4
    ROUND = 12582912.0
    EPS_LN = 1e-5
    assert F == P and T % (2 * Q) == 0

    x_v = x.rearrange("(t p) f -> p t f", p=P)
    out_v = out.rearrange("(t p) f -> p t f", p=P)
    adj_v = adj_t.rearrange("(t p) i -> p t i", p=P)
    x1_d = nc.dram_tensor("x1_d", (N, F), F32).ap().rearrange("(t p) f -> p t f", p=P)
    h1_d = nc.dram_tensor("h1_d", (N, F), F32).ap().rearrange("(t p) f -> p t f", p=P)
    sup_d = nc.dram_tensor("sup_d", (N, F), F32).ap().rearrange("(t p) f -> p t f", p=P)
    att_d = nc.dram_tensor("att_d", (N, H * F), F32).ap().rearrange("(t p) f -> p t f", p=P)
    row_d = nc.dram_tensor("row_d", (T, H, P), BF16).ap()

    main = ExitStack()
    with main:
        def sem(name):
            return main.enter_context(nc.semaphore(name))

        def sb(name, shape, dt, ctx=main):
            return ctx.enter_context(nc.sbuf_tensor(name, shape, dt))

        def ps(name, shape, ctx, dt=F32):
            return ctx.enter_context(nc.psum_tensor(name, shape, dt))

        ident = sb("ident", [P, P], F32)

        def run_chunks(eng, first, rest, drain):
            first(0)
            rest(0)
            if C > 2:
                with eng.Fori(0, C // 2 - 1) as cp:
                    for half in range(2):
                        c = 2 * cp + half + 1
                        first(c)
                        drain(c - 1, half)
                        rest(c)
            first(C - 1)
            drain(C - 2, 0)
            rest(C - 1)
            drain(C - 1, 1)

        def layer_norm_relu(v, step, xs, xc, sq, mean, var, std, rstd, act_sqrt, act_done):
            step(v.tensor_reduce(mean[:, :], xs[:, :, :], AX.X, ALU.add))
            step(v.tensor_scalar(mean[:, :], mean[:, :], 1.0 / F, None, ALU.mult))
            step(v.tensor_tensor(xc[:, :, :], xs[:, :, :],
                                 mean[:, :].unsqueeze(2).to_broadcast([P, T, F]), ALU.subtract))
            step(v.tensor_tensor(sq[:, :, :], xc[:, :, :], xc[:, :, :], ALU.mult))
            step(v.tensor_reduce(var[:, :], sq[:, :, :], AX.X, ALU.add))
            v.tensor_scalar(var[:, :], var[:, :], 1.0 / F, EPS_LN, ALU.mult, ALU.add)\
                .then_inc(act_sqrt, 1)
            v.wait_ge(act_done, 1)
            v.wait_ge(act_sqrt, 1)
            step(v.reciprocal(rstd[:, :], std[:, :]))
            step(v.tensor_tensor(rstd[:, :], rstd[:, :], var[:, :], ALU.mult))
            step(v.tensor_tensor(std[:, :], std[:, :], rstd[:, :], ALU.add))
            step(v.tensor_scalar(std[:, :], std[:, :], 0.5, None, ALU.mult))
            step(v.reciprocal(rstd[:, :], std[:, :]))

        dn = sb("dn", [P, T], F32)
        kb = sb("kb", [P, H, T], F32)
        g_all = sb("g_all", [P, H, T], F32)
        pw = sb("pw", [P, T, H], BF16)
        mask_scope = ExitStack()
        main.enter_context(mask_scope)
        mask = sb("mask", [P, T, N], U8, mask_scope)

        o0_scope = ExitStack()
        main.enter_context(o0_scope)
        o0 = sb("o0", [P, T, F], F32, o0_scope)

        with ExitStack() as l0:
            hx = sb("hx", [P, T, F1], F32, l0)
            scal = sb("scal", [P, 8, T], F32, l0)
            a_src, a_dst, es, es2, nes, eps, t0, t1 = (scal[:, k, :] for k in range(8))
            rrow = sb("rrow", [P, N], F32, l0)

            with ExitStack() as p0:
                xs = o0
                xc = sb("xc", [P, T, F], F32, p0)
                st = sb("st", [P, 4, T], F32, p0)
                mean, var, std, rstd = (st[:, k, :] for k in range(4))
                w0_s = sb("w0_s", [P, F], F32, p0)
                w0t_s = sb("w0t_s", [P, F], F32, p0)
                att_s = sb("att_s", [P, 2], F32, p0)
                u_s = sb("u_s", [P, 2], F32, p0)
                udst = sb("udst", [P, P], F32, p0)
                h0 = sb("h0", [P, Q, F], F32, p0)
                h0t = sb("h0t", [P, CW], F32, p0)
                amax = sb("amax", [P, 2], F32, p0)
                p_u = ps("p_u", [P, 512], p0)
                p_t = ps("p_t", [P, 512], p0)
                p_h = ps("p_h", [P, Q, F], p0)
                p_ad = ps("p_ad", [P, 512], p0)
                p_d = ps("p_d", [P, CW], p0)
                loaded, steps = sem("a_loaded"), sem("a_steps")
                var_ready, root_ready = sem("a_var_ready"), sem("a_root_ready")
                id_ready, u_ready, u_copied = sem("a_id"), sem("a_u_ready"), sem("a_u_copied")
                h0_ready, h0_turned = sem("a_h0_ready"), sem("a_h0_turned")
                h0t_ready, h_done = sem("a_h0t_ready"), sem("a_h_done")
                h_copied, d_copied = sem("a_h_copied"), sem("a_d_copied")
                rowmax, allmax = sem("a_rowmax"), sem("a_allmax")
                exp_in, exp_out = sem("a_exp_in"), sem("a_exp_out")
                block = p0.enter_context(nc.Block())

                @block.sync
                def _(sp):
                    sp.dma_start(xs[:, :, :], x_v).then_inc(loaded, 16)
                    sp.dma_start(w0_s[:, :], w0).then_inc(loaded, 16)
                    sp.dma_start(w0t_s[:, :], w0_t).then_inc(loaded, 16)
                    sp.dma_start(att_s[:, 0:1], att_src.rearrange("a f -> f a")).then_inc(loaded, 16)
                    sp.dma_start(att_s[:, 1:2], att_dst.rearrange("a f -> f a")).then_inc(loaded, 16)

                @block.gpsimd
                def _(pool):
                    pool.memset(ident[:, :], 0.0).then_inc(id_ready, 1)
                    pool.wait_ge(id_ready, 1)
                    pool.affine_select(out=ident[:, :], in_=ident[:, :], compare_op=ALU.not_equal, fill=1.0,
                                       base=0, pattern=[[-1, P]], channel_multiplier=1).then_inc(id_ready, 1)
                    pool.wait_ge(rowmax, 1)
                    pool.partition_all_reduce(amax[:, 1:2], amax[:, 0:1], P,
                                              bass.bass_isa.ReduceOp.max).then_inc(allmax, 1)

                @block.tensor
                def _(pe):
                    pe.sem_inc(h0_turned, 1)
                    pe.sem_inc(h_done, 1)
                    pe.wait_ge(loaded, 80)
                    pe.matmul(p_u[:, 0:2], w0_s[:, :], att_s[:, :], start=True, stop=True).then_inc(u_ready, 1)
                    pe.wait_ge(id_ready, 2)
                    pe.wait_ge(u_copied, 2)
                    with pe.Fori(0, NG) as q:
                        pe.wait_ge(h0_ready, q + 1)
                        pe.wait_ge(h0t_ready, 1 + q)
                        for k in range(Q):
                            last = pe.transpose(p_t[:, k * P:(k + 1) * P], h0[:, k, :], ident[:, :])
                        last.then_inc(h0_turned, 1)
                        pe.wait_ge(h0t_ready, 1 + q + 1)
                        pe.wait_ge(h_copied, 1 + q)
                        pe.wait_ge(d_copied, 1 + q)
                        for k in range(Q):
                            t = h0t[:, k * P:(k + 1) * P]
                            pe.matmul(p_h[:, k, :], t, w0t_s[:, :], start=True, stop=True)
                            pe.matmul(p_ad[:, 2 * k:2 * k + 2], t, u_s[:, :], start=True, stop=True)
                        pe.matmul(p_d[:, :], udst[:, :], h0t[:, :], start=True, stop=True).then_inc(h_done, 1)

                @block.scalar
                def _(act):
                    act.sem_inc(h0t_ready, 1)
                    act.sem_inc(d_copied, 1)
                    act.wait_ge(var_ready, 1)
                    act.activation(std, var, ACT.Sqrt).then_inc(root_ready, 1)
                    with act.Fori(0, NG) as q:
                        act.wait_ge(h0_turned, 1 + q + 1)
                        act.nop(nofuse=True)
                        act.wait_ge(h_done, 1 + q)
                        act.nop(nofuse=True)
                        act.activation(h0t[:, :], p_t[:, :], ACT.Copy).then_inc(h0t_ready, 1)
                        act.wait_ge(h_done, 1 + q + 1)
                        act.nop(nofuse=True)
                        act.activation(rrow[:, ds(q * CW, CW)], p_d[:, :], ACT.Copy).then_inc(d_copied, 1)
                    act.wait_ge(exp_in, 1)
                    act.activation(es, t0, ACT.Exp).then_inc(exp_out, 1)
                    act.activation(es2, t0, ACT.Exp, scale=0.2).then_inc(exp_out, 1)
                    act.wait_ge(exp_in, 2)
                    act.activation(eps, t1, ACT.Exp).then_inc(exp_out, 1)
                    act.wait_ge(exp_in, 3)
                    act.activation(rrow[:, :], rrow[:, :], ACT.Exp).then_inc(exp_out, 1)

                @block.vector
                def _(v):
                    step = Steps(v, steps)
                    v.sem_inc(h_copied, 1)
                    v.wait_ge(loaded, 80)
                    v.wait_ge(u_ready, 1)
                    v.tensor_copy(u_s[:, :], p_u[:, 0:2]).then_inc(u_copied, 1)
                    v.wait_ge(u_copied, 1)
                    v.tensor_copy(udst[:, :], u_s[:, 1:2].to_broadcast([P, P])).then_inc(u_copied, 1)
                    sq = rrow[:, :].rearrange("p (t f) -> p t f", f=F)
                    layer_norm_relu(v, step, xs, xc, sq, mean, var, std, rstd, var_ready, root_ready)
                    with v.Fori(0, NG) as q:
                        v.wait_ge(h0_turned, 1 + q)
                        v.scalar_tensor_tensor(
                            h0[:, :, :], xc[:, ds(q * Q, Q), :], 0.0,
                            rstd[:, ds(q * Q, Q)].unsqueeze(2).to_broadcast([P, Q, F]),
                            ALU.max, ALU.mult).then_inc(h0_ready, 1)
                        v.wait_ge(h_done, 1 + q + 1)
                        v.tensor_copy(hx[:, ds(q * Q, Q), 0:F], p_h[:, :, :])
                        pair = p_ad[:, 0:2 * Q].rearrange("p (k two) -> p k two", two=2)
                        v.tensor_copy(a_src[:, ds(q * Q, Q)], pair[:, :, 0])
                        v.tensor_copy(a_dst[:, ds(q * Q, Q)], pair[:, :, 1]).then_inc(h_copied, 1)
                    v.wait_ge(h_copied, 1 + NG)
                    step(v.memset(hx[:, :, F:F1], 1.0))
                    v.tensor_reduce(amax[:, 0:1], a_src, AX.X, ALU.max).then_inc(rowmax, 1)
                    v.wait_ge(allmax, 1)
                    v.tensor_scalar(t0, a_src, amax[:, 1:2], None, ALU.subtract).then_inc(exp_in, 1)
                    step(v.tensor_scalar(a_dst, a_dst, amax[:, 1:2], None, ALU.add))
                    step(v.tensor_scalar(t1, a_dst, 0.8, 80.0, ALU.mult, ALU.add))
                    step(v.tensor_scalar(t1, t1, 0.0, None, ALU.min))
                    v.tensor_tensor(t1, t1, a_dst, ALU.subtract).then_inc(exp_in, 1)
                    v.wait_ge(d_copied, 1 + NG)
                    step(v.tensor_scalar(rrow[:, :], rrow[:, :], amax[:, 1:2], -0.8, ALU.add, ALU.mult))
                    v.tensor_scalar(rrow[:, :], rrow[:, :], 80.0, None, ALU.min).then_inc(exp_in, 1)
                    v.wait_ge(exp_out, 1)
                    step(v.tensor_scalar(nes, es, -1.0, None, ALU.mult))
                    v.wait_ge(exp_out, 3)
                    step(v.tensor_scalar(eps, eps, 1e-8, None, ALU.mult))

            with ExitStack() as p1:
                JG, SL = 2, 4
                G4 = T // (JG * SL)
                OFF = 8
                adj = sb("adj", [P, SL, JG, CW], F32, p1)
                rel = sb("rel", [P, 2, CW], F32, p1)
                w = sb("w", [P, 4, CW], F32, p1)
                rden = sb("rden", [P, 2, Q], F32, p1)
                zero = sb("zero", [P, 2, P], BF16, p1)
                acc = [ps(f"acc{k}", [P, Q, 512], p1) for k in range(2)]
                adj_in = [sem(f"b_adj_in{k}") for k in range(SL)]
                rel_done, w_done = sem("b_rel_done"), sem("b_w_done")
                mask_done, mm_done = sem("b_mask_done"), sem("b_mm_done")
                chunk_done, drained = sem("b_chunk_done"), sem("b_drained")
                steps, zeroed = sem("b_steps"), sem("b_zeroed")
                block = p1.enter_context(nc.Block())

                @block.sync
                def _(sp):
                    with sp.Fori(0, C) as c:
                        with sp.Fori(0, G4) as r:
                            for u in range(SL):
                                n = (c * G4 + r) * SL + u
                                used = sp.snap(OFF + JG * (n - SL + 1))
                                kept = sp.snap(OFF + n - SL + 1)
                                sp.wait_ge(w_done, used)
                                sp.nop(nofuse=True)
                                sp.wait_ge(mask_done, kept)
                                sp.dma_start(adj[:, u, :, :],
                                             adj_v[:, ds((r * SL + u) * JG, JG), ds(c * CW, CW)])\
                                    .then_inc(adj_in[u], 16)

                @block.gpsimd
                def _(pool):
                    pool.memset(zero[:, :, :], 0.0).then_inc(zeroed, 1)
                    pool.sem_inc(mask_done, OFF)
                    with pool.Fori(0, C) as c:
                        with pool.Fori(0, G4) as r:
                            for u in range(SL):
                                pool.wait_ge(adj_in[u], 16 * (c * G4 + r + 1))
                                pool.tensor_copy(mask[:, ds((r * SL + u) * JG, 1), ds(c * CW, CW)],
                                                 adj[:, u, 0:1, :]).then_inc(mask_done, 1)

                @block.scalar
                def _(act):
                    act.sem_inc(rel_done, OFF)
                    with act.Fori(0, C) as c:
                        with act.Fori(0, G4) as r:
                            for u in range(SL):
                                for jt in range(JG):
                                    k = ((c * G4 + r) * SL + u) * JG + jt
                                    j = (r * SL + u) * JG + jt
                                    act.wait_ge(w_done, OFF + k - 1)
                                    act.nop(nofuse=True)
                                    act.activation(rel[:, jt, :], rrow[:, ds(c * CW, CW)], ACT.Relu,
                                                   bias=nes[:, ds(j, 1)], scale=es2[:, ds(j, 1)])\
                                       .then_inc(rel_done, 1)

                @block.vector
                def _(v):
                    v.sem_inc(w_done, OFF)
                    v.sem_inc(drained, 2)

                    def weights(c, r):
                        for u in range(SL):
                            v.wait_ge(adj_in[u], 16 * (c * G4 + r + 1))
                            v.tensor_copy(mask[:, ds((r * SL + u) * JG + 1, JG - 1), ds(c * CW, CW)],
                                          adj[:, u, 1:JG, :])
                            for jt in range(JG):
                                k = ((c * G4 + r) * SL + u) * JG + jt
                                j = (r * SL + u) * JG + jt
                                v.wait_ge(rel_done, OFF + k + 1)
                                v.wait_ge(mm_done, OFF + k - 3)
                                v.scalar_tensor_tensor(w[:, (u * JG + jt) % 4, :], rel[:, jt, :],
                                                       es[:, ds(j, 1)], adj[:, u, jt, :],
                                                       ALU.add, ALU.mult).then_inc(w_done, 1)

                    def rest(c):
                        if G4 > 1:
                            with v.Fori(1, G4) as r:
                                weights(c, r)

                    def drain(c, half):
                        a = acc[half]
                        step = Steps(v, steps, c * 2)
                        v.wait_ge(drained, 2 + c)
                        v.wait_ge(chunk_done, c + 1)
                        step(v.tensor_tensor(rden[:, 0, :], a[:, :, F], eps[:, ds(c * Q, Q)], ALU.add))
                        step(v.reciprocal(rden[:, 1, :], rden[:, 0, :]))
                        v.tensor_tensor(o0[:, ds(c * Q, Q), :], a[:, :, 0:F],
                                        rden[:, 1, :].unsqueeze(2).to_broadcast([P, Q, F]),
                                        ALU.mult).then_inc(drained, 1)

                    run_chunks(v, lambda c: weights(c, 0), rest, drain)

                @block.tensor
                def _(pe):
                    pe.sem_inc(mm_done, OFF)
                    pe.wait_ge(zeroed, 1)
                    with pe.Fori(0, C // 2) as cp:
                        for half in range(2):
                            c = 2 * cp + half
                            pe.wait_ge(drained, 2 + c - 1)
                            for it in range(Q):
                                pe.matmul(acc[half][:, it, 0:P], zero[:, 0, :], zero[:, 1, :],
                                          start=True, stop=False, skip_group_check=True)
                                pe.matmul(acc[half][:, it, P:P + 1], zero[:, 0, :], zero[:, 1, 0:1],
                                          start=False, stop=False, skip_group_check=True)
                            with pe.Fori(0, G4) as r:
                                for u in range(SL):
                                    for jt in range(JG):
                                        k = ((c * G4 + r) * SL + u) * JG + jt
                                        j = (r * SL + u) * JG + jt
                                        pe.wait_ge(w_done, OFF + k + 1)
                                        for it in range(Q):
                                            last = pe.matmul(acc[half][:, it, 0:F1],
                                                             w[:, (u * JG + jt) % 4, it * P:(it + 1) * P],
                                                             hx[:, ds(j, 1), :].rearrange("p a f -> p (a f)"),
                                                             start=False, stop=False, skip_group_check=True)
                                        last.then_inc(mm_done, 1)
                            for it in range(Q):
                                last = pe.matmul(acc[half][:, it, 0:P], zero[:, 0, :], zero[:, 1, :],
                                                 start=False, stop=True, skip_group_check=True)
                            last.then_inc(chunk_done, 1)

        with ExitStack() as l1a:
            h2 = sb("h2", [P, T, 2, F], F16, l1a)
            with ExitStack() as p2:
                xs = sb("xs2", [P, T, F], F32, p2)
                xc = sb("xc2", [P, T, F], F32, p2)
                st = sb("st2", [P, 4, T], F32, p2)
                mean, var, std, rstd = (st[:, k, :] for k in range(4))
                off = sb("off", [P, P], BF16, p2)
                loaded, steps = sem("c_loaded"), sem("c_steps")
                var_ready, root_ready = sem("c_var_ready"), sem("c_root_ready")
                neg_ready, exp_ready = sem("c_neg_ready"), sem("c_exp_ready")
                x1_ready, h1_ready, stored = sem("c_x1_ready"), sem("c_h1_ready"), sem("c_stored")
                off_ready, cleared = sem("c_off_ready"), sem("c_cleared")
                block = p2.enter_context(nc.Block())

                @block.sync
                def _(sp):
                    sp.dma_start(xs[:, :, :], x_v).then_inc(loaded, 16)
                    with nc.allow_non_contiguous_dma(reason="a matrix's diagonal has no run"):
                        diag = bass.AP(tensor=adj_t.tensor, offset=0, ap=[[N + 1, P], [P * (N + 1), T], [1, 1]])
                        sp.dma_start(dn[:, :].unsqueeze(2), diag).then_inc(loaded, 16)
                    sp.wait_ge(x1_ready, 1)
                    sp.dma_start(x1_d, xs[:, :, :]).then_inc(stored, 16)
                    sp.wait_ge(h1_ready, 1)
                    sp.dma_start(h1_d, xc[:, :, :]).then_inc(stored, 16)
                    sp.wait_ge(stored, 32)
                    sp.wait_ge(loaded, 32)

                @block.gpsimd
                def _(pool):
                    pool.memset(off[:, :], 1.0).then_inc(off_ready, 1)
                    pool.wait_ge(off_ready, 1)
                    pool.affine_select(out=off[:, :], in_=off[:, :], compare_op=ALU.not_equal, fill=0.0,
                                       base=0, pattern=[[-1, P]], channel_multiplier=1).then_inc(off_ready, 1)

                @block.scalar
                def _(act):
                    act.wait_ge(neg_ready, 1)
                    act.activation(xc[:, :, :], xc[:, :, :], ACT.Exp).then_inc(exp_ready, 1)
                    act.wait_ge(var_ready, 1)
                    act.activation(std, var, ACT.Sqrt).then_inc(root_ready, 1)

                @block.vector
                def _(v):
                    step = Steps(v, steps)
                    v.tensor_scalar(xc[:, :, :], o0[:, :, :], 0.0, None, ALU.min).then_inc(neg_ready, 1)
                    step(v.tensor_scalar(o0[:, :, :], o0[:, :, :], 0.0, -1.0, ALU.max, ALU.add))
                    v.wait_ge(exp_ready, 1)
                    step(v.tensor_tensor(o0[:, :, :], o0[:, :, :], xc[:, :, :], ALU.add))
                    v.wait_ge(loaded, 32)
                    v.tensor_tensor(xs[:, :, :], xs[:, :, :], o0[:, :, :], ALU.add).then_inc(x1_ready, 1)
                    v.wait_ge(x1_ready, 1)
                    layer_norm_relu(v, step, xs, xc, o0, mean, var, std, rstd, var_ready, root_ready)
                    v.scalar_tensor_tensor(xc[:, :, :], xc[:, :, :], 0.0,
                                           rstd.unsqueeze(2).to_broadcast([P, T, F]),
                                           ALU.max, ALU.mult).then_inc(h1_ready, 1)
                    v.wait_ge(h1_ready, 1)
                    step(v.tensor_scalar(h2[:, :, 0, :], xc[:, :, :], SPLIT, None, ALU.mult))
                    step(v.scalar_tensor_tensor(h2[:, :, 1, :], xc[:, :, :], SPLIT, h2[:, :, 0, :],
                                                ALU.mult, ALU.subtract))
                    v.wait_ge(off_ready, 2)
                    with v.Fori(0, T) as t:
                        block_t = mask[:, ds(t, 1), ds(t * P, P)].rearrange("p a i -> p (a i)")
                        v.tensor_tensor(block_t, block_t, off[:, :], ALU.mult).then_inc(cleared, 1)
                    v.wait_ge(cleared, T)

            sup = o0
            with ExitStack() as p3:
                JG, SL = 2, 4
                G4 = T // (JG * SL)
                OFF = SL
                m16 = sb("m16", [P, SL, JG, CW], BF16, p3)
                high = sb("high", [P, Q, F], F32, p3)
                zero = sb("zero3", [P, 2, 2 * F], BF16, p3)
                acc = [ps(f"sacc{k}", [P, Q, 512], p3) for k in range(2)]
                m_done = [sem(f"d_mask{u}") for u in range(SL)]
                mm_done, chunk_done = sem("d_mm_done"), sem("d_chunk_done")
                drained, high_done, zeroed = sem("d_drained"), sem("d_high_done"), sem("d_zeroed")
                block = p3.enter_context(nc.Block())

                @block.gpsimd
                def _(pool):
                    pool.memset(zero[:, :, :], 0.0).then_inc(zeroed, 1)

                @block.scalar
                def _(act):
                    def even(c, r):
                        for u in range(0, SL, 2):
                            act.wait_ge(mm_done, (c * G4 + r) * SL + u + 1)
                            act.nop(nofuse=True)
                            act.activation(m16[:, u, :, :], mask[:, ds((r * SL + u) * JG, JG), ds(c * CW, CW)],
                                           ACT.Copy).then_inc(m_done[u], 1)

                    def rest(c):
                        if G4 > 1:
                            with act.Fori(1, G4) as r:
                                even(c, r)

                    def drain(c, half):
                        act.wait_ge(chunk_done, c + 1)
                        act.nop(nofuse=True)
                        act.wait_ge(drained, 2 + c)
                        act.nop(nofuse=True)
                        act.activation(high[:, :, :], acc[half][:, :, 0:F], ACT.Copy,
                                       scale=1.0 / SPLIT).then_inc(high_done, 1)

                    run_chunks(act, lambda c: even(c, 0), rest, drain)

                @block.vector
                def _(v):
                    v.sem_inc(drained, 2)

                    def odd(c, r):
                        for u in range(1, SL, 2):
                            v.wait_ge(mm_done, (c * G4 + r) * SL + u + 1)
                            v.tensor_copy(m16[:, u, :, :], mask[:, ds((r * SL + u) * JG, JG), ds(c * CW, CW)])\
                                .then_inc(m_done[u], 1)

                    def rest(c):
                        if G4 > 1:
                            with v.Fori(1, G4) as r:
                                odd(c, r)

                    def drain(c, half):
                        v.wait_ge(high_done, c + 1)
                        v.scalar_tensor_tensor(sup[:, ds(c * Q, Q), :], acc[half][:, :, F:2 * F], 1.0 / SPLIT,
                                               high[:, :, :], ALU.mult, ALU.add).then_inc(drained, 1)

                    run_chunks(v, lambda c: odd(c, 0), rest, drain)

                @block.tensor
                def _(pe):
                    pe.sem_inc(mm_done, OFF)
                    pe.wait_ge(zeroed, 1)
                    with pe.Fori(0, C // 2) as cp:
                        for half in range(2):
                            c = 2 * cp + half
                            pe.wait_ge(drained, 2 + c - 1)
                            for it in range(Q):
                                pe.matmul(acc[half][:, it, 0:2 * F], zero[:, 0, 0:P], zero[:, 1, :],
                                          start=True, stop=False, skip_group_check=True)
                            with pe.Fori(0, G4) as r:
                                for u in range(SL):
                                    pe.wait_ge(m_done[u], c * G4 + r + 1)
                                    for jt in range(JG):
                                        j = (r * SL + u) * JG + jt
                                        for it in range(Q):
                                            last = pe.matmul(acc[half][:, it, 0:2 * F],
                                                             m16[:, u, jt, it * P:(it + 1) * P],
                                                             h2[:, ds(j, 1), :, :].rearrange("p a s f -> p (a s f)"),
                                                             start=False, stop=False, skip_group_check=True)
                                    last.then_inc(mm_done, 1)
                            for it in range(Q):
                                last = pe.matmul(acc[half][:, it, 0:2 * F], zero[:, 0, 0:P], zero[:, 1, :],
                                                 start=False, stop=True, skip_group_check=True)
                            last.then_inc(chunk_done, 1)

        with ExitStack() as p4:
            e_all = sb("e_all", [P, T, H], F32, p4)
            d_all = sb("d_all", [P, H, T], F32, p4)
            gwt = sb("gwt", [P, H, F], F32, p4)
            ga = sb("ga", [P, H], F32, p4)
            wa = sb("wa", [P, H], F32, p4)
            sg = sb("sg", [P, Q, F], F32, p4)
            sgt = sb("sgt", [P, CW], F32, p4)
            mx = sb("mx", [P, 2, H], F32, p4)
            b76 = sb("b76", [P, 1], F32, p4)
            kf = sb("kf", [P, H, T], F32, p4)
            p_wa = ps("p_wa", [P, 512], p4)
            p_t = ps("p_t4", [P, 512], p4)
            p_e = ps("p_e", [P, 512], p4)
            loaded, stored, steps = sem("e_loaded"), sem("e_stored"), sem("e_steps")
            wa_done, wa_copied = sem("e_wa_done"), sem("e_wa_copied")
            sg_ready, sg_turned, sgt_ready = sem("e_sg_ready"), sem("e_sg_turned"), sem("e_sgt_ready")
            e_done, e_copied = sem("e_done"), sem("e_copied")
            rowmax, allmax = sem("e_rowmax"), sem("e_allmax")
            exp_in, exp_out = sem("e_exp_in"), sem("e_exp_out")
            block = p4.enter_context(nc.Block())

            @block.sync
            def _(sp):
                sp.dma_start(gwt[:, :, :], gat_w_t.rearrange("h g f -> g h f")).then_inc(loaded, 16)
                with nc.allow_non_contiguous_dma(reason="three short vectors"):
                    sp.dma_start(ga[:, :], gat_a[:, 0:F, 0].rearrange("h f -> f h")).then_inc(loaded, 16)
                sp.dma_start(sup_d, sup[:, :, :]).then_inc(stored, 16)
                sp.wait_ge(stored, 16)

            @block.gpsimd
            def _(pool):
                pool.wait_ge(rowmax, 1)
                pool.partition_all_reduce(mx[:, 1, :], mx[:, 0, :], P,
                                          bass.bass_isa.ReduceOp.max).then_inc(allmax, 1)

            @block.tensor
            def _(pe):
                pe.sem_inc(sg_turned, 1)
                pe.sem_inc(e_done, 1)
                pe.wait_ge(loaded, 32)
                for k in range(H):
                    last = pe.matmul(p_wa[:, k:k + 1], gwt[:, k, :], ga[:, k:k + 1], start=True, stop=True)
                last.then_inc(wa_done, 1)
                pe.wait_ge(wa_copied, 1)
                with pe.Fori(0, NG) as q:
                    pe.wait_ge(sg_ready, q + 1)
                    for k in range(Q):
                        last = pe.transpose(p_t[:, k * P:(k + 1) * P], sg[:, k, :], ident[:, :])
                    last.then_inc(sg_turned, 1)
                    pe.wait_ge(sgt_ready, q + 1)
                    pe.wait_ge(e_copied, 1 + q)
                    for k in range(Q):
                        last = pe.matmul(p_e[:, H * k:H * (k + 1)], sgt[:, k * P:(k + 1) * P], wa[:, :],
                                         start=True, stop=True)
                    last.then_inc(e_done, 1)

            @block.scalar
            def _(act):
                with act.Fori(0, NG) as q:
                    act.wait_ge(sg_turned, 1 + q + 1)
                    act.nop(nofuse=True)
                    act.wait_ge(e_done, 1 + q)
                    act.nop(nofuse=True)
                    act.activation(sgt[:, :], p_t[:, :], ACT.Copy).then_inc(sgt_ready, 1)
                act.wait_ge(exp_in, 1)
                act.activation(pw[:, :, :].rearrange("p t h -> p h t"), d_all[:, :, :], ACT.Exp,
                               bias=b76[:, 0:1], scale=1.0 / 16).then_inc(exp_out, 1)
                act.wait_ge(exp_in, 2)
                act.activation(g_all[:, :, :], g_all[:, :, :], ACT.Exp).then_inc(exp_out, 1)

            @block.vector
            def _(v):
                step = Steps(v, steps)
                v.sem_inc(e_copied, 1)
                step(v.memset(b76[:, :], 76.0))
                v.wait_ge(wa_done, 1)
                v.tensor_copy(wa[:, :], p_wa[:, 0:H]).then_inc(wa_copied, 1)
                with v.Fori(0, NG) as q:
                    v.wait_ge(sg_turned, 1 + q)
                    v.tensor_copy(sg[:, :, :], sup[:, ds(q * Q, Q), :]).then_inc(sg_ready, 1)
                    v.wait_ge(e_done, 1 + q + 1)
                    v.tensor_copy(e_all[:, ds(q * Q, Q), :],
                                  p_e[:, 0:Q * H].rearrange("p (k h) -> p k h", h=H)).then_inc(e_copied, 1)
                v.wait_ge(e_copied, 1 + NG)
                step(v.scalar_tensor_tensor(e_all[:, :, :], e_all[:, :, :], 0.2, e_all[:, :, :],
                                            ALU.mult, ALU.max))
                v.tensor_reduce(mx[:, 0, :], e_all[:, :, :].rearrange("p t h -> p h t"), AX.X, ALU.max)\
                    .then_inc(rowmax, 1)
                v.wait_ge(allmax, 1)
                v.tensor_tensor(d_all[:, :, :], e_all[:, :, :].rearrange("p t h -> p h t"),
                                mx[:, 1, :].unsqueeze(2).to_broadcast([P, H, T]),
                                ALU.subtract).then_inc(exp_in, 1)
                v.wait_ge(exp_in, 1)
                step(v.tensor_scalar(kf[:, :, :], d_all[:, :, :], LOG2E, ROUND, ALU.mult, ALU.add))
                step(v.tensor_scalar(kf[:, :, :], kf[:, :, :], ROUND, None, ALU.subtract))
                step(v.scalar_tensor_tensor(g_all[:, :, :], kf[:, :, :], -LN2_HI, d_all[:, :, :],
                                            ALU.mult, ALU.add))
                v.scalar_tensor_tensor(g_all[:, :, :], kf[:, :, :], -LN2_LO, g_all[:, :, :],
                                       ALU.mult, ALU.add).then_inc(exp_in, 1)
                step(v.tensor_scalar(kb[:, :, :], kf[:, :, :], 128.0, 128.0 * 1969 - 262144.0,
                                     ALU.mult, ALU.add))
                v.wait_ge(exp_out, 2)
                step(v.tensor_scalar(g_all[:, :, :], g_all[:, :, :], SPLIT, None, ALU.mult))

        o0_scope.close()

        with ExitStack() as l1:
            xh = sb("xh", [P, H, T, 2, F1], F16, l1)
            with ExitStack() as p5:
                JG, SL = 2, 4
                G4 = T // (JG * SL)
                OFF = SL
                TH = T * H
                m16 = sb("m16b", [P, SL, JG, CW], BF16, p5)
                zero = sb("zero5", [P, 2, P], BF16, p5)
                hg = sb("hg", [P, 2, Q, F], F32, p5)
                gx = sb("gx", [P, H, Q, F], F32, p5)
                rs = sb("rs", [P, TH], F32, p5)
                rsi = sb("rsi", [P, TH], I32, p5)
                rt = sb("rt", [TH, P], BF16, p5)
                p_r = ps("p_r", [P, 512], p5)
                p_rt = ps("p_rt", [P, 512], p5)
                m_done = [sem(f"f_mask{u}") for u in range(SL)]
                mm_done, zeroed, sums_done = sem("f_mm_done"), sem("f_zeroed"), sem("f_sums_done")
                steps, turned, rows_ready, stored = sem("f_steps"), sem("f_turned"), sem("f_rows_ready"), sem("f_stored")
                scale_ready = sem("f_scale_ready")
                h_in = [sem("f_h_in0"), sem("f_h_in1")]
                gx_ready, hi_ready, lo_ready = sem("f_gx_ready"), sem("f_hi_ready"), sem("f_lo_ready")
                block = p5.enter_context(nc.Block())

                @block.sync
                def _(sp):
                    with sp.Fori(0, NG // 2) as qp:
                        for s in range(2):
                            q = 2 * qp + s
                            sp.wait_ge(lo_ready, 2 * H + (q - 1) * H)
                            sp.dma_start(hg[:, s, :, :], h1_d[:, ds(q * Q, Q), :]).then_inc(h_in[s], 16)
                    sp.wait_ge(rows_ready, 1)
                    sp.dma_start(row_d.rearrange("t h p -> (t h) p"), rt[:, :]).then_inc(stored, 16)
                    sp.wait_ge(stored, 16)

                @block.gpsimd
                def _(pool):
                    pool.memset(zero[:, :, :], 0.0).then_inc(zeroed, 1)

                @block.scalar
                def _(act):
                    with act.Fori(0, C) as c:
                        with act.Fori(0, G4) as r:
                            for u in range(0, SL, 2):
                                act.wait_ge(mm_done, (c * G4 + r) * SL + u + 1)
                                act.nop(nofuse=True)
                                act.activation(m16[:, u, :, :],
                                               mask[:, ds((r * SL + u) * JG, JG), ds(c * CW, CW)],
                                               ACT.Copy).then_inc(m_done[u], 1)
                        for k in range(H):
                            act.wait_ge(gx_ready, c * H + k + 1)
                            act.nop(nofuse=True)
                            act.activation(xh[:, k, ds(c * Q, Q), 0, 0:F], gx[:, k, :, :],
                                           ACT.Copy).then_inc(hi_ready, 1)
                    act.wait_ge(turned, 1)
                    act.activation(rt[:, :], p_rt[0:TH, 0:P], ACT.Copy).then_inc(rows_ready, 1)

                @block.vector
                def _(v):
                    v.sem_inc(lo_ready, 2 * H)
                    with v.Fori(0, C // 2) as cp:
                        for s in range(2):
                            c = 2 * cp + s
                            v.wait_ge(h_in[s], 16 * (cp + 1))
                            v.wait_ge(lo_ready, (c + 2) * H)
                            for k in range(H):
                                v.tensor_tensor(gx[:, k, :, :], hg[:, s, :, :],
                                                g_all[:, k, ds(c * Q, Q)].unsqueeze(2).to_broadcast([P, Q, F]),
                                                ALU.mult).then_inc(gx_ready, 1)
                            with v.Fori(0, G4) as r:
                                for u in range(1, SL, 2):
                                    v.wait_ge(mm_done, (c * G4 + r) * SL + u + 1)
                                    v.tensor_copy(m16[:, u, :, :],
                                                  mask[:, ds((r * SL + u) * JG, JG), ds(c * CW, CW)])\
                                        .then_inc(m_done[u], 1)
                            for k in range(H):
                                v.wait_ge(hi_ready, c * H + k + 1)
                                v.tensor_tensor(xh[:, k, ds(c * Q, Q), 1, 0:F], gx[:, k, :, :],
                                                xh[:, k, ds(c * Q, Q), 0, 0:F],
                                                ALU.subtract).then_inc(lo_ready, 1)
                    step = Steps(v, steps)
                    step(v.tensor_copy(xh[:, :, :, 0, F], g_all[:, :, :]))
                    step(v.tensor_tensor(xh[:, :, :, 1, F], g_all[:, :, :], xh[:, :, :, 0, F], ALU.subtract))
                    v.wait_ge(sums_done, 1)
                    step(v.tensor_copy(rs[:, :], p_r[:, 0:TH]))
                    step(v.tensor_scalar(rsi[:, :], rs[:, :].bitcast(I32), 23, None, ALU.logical_shift_right))
                    v.tensor_scalar(rs[:, :], rsi[:, :], -2048.0, 2048.0 * 255, ALU.mult, ALU.add)\
                        .then_inc(scale_ready, 1)

                @block.tensor
                def _(pe):
                    pe.sem_inc(mm_done, OFF)
                    pe.wait_ge(zeroed, 1)
                    pe.matmul(p_r[:, 0:TH], zero[:, 0, :], zero[:, 1, 0:TH], start=True, stop=False,
                              skip_group_check=True)
                    with pe.Fori(0, C) as c:
                        with pe.Fori(0, G4) as r:
                            for u in range(SL):
                                pe.wait_ge(m_done[u], c * G4 + r + 1)
                                for jt in range(JG):
                                    j = (r * SL + u) * JG + jt
                                    for it in range(Q):
                                        last = pe.matmul(p_r[:, ds((c * Q + it) * H, H)],
                                                         m16[:, u, jt, it * P:(it + 1) * P],
                                                         pw[:, ds(j, 1), :].rearrange("p a h -> p (a h)"),
                                                         start=False, stop=False, skip_group_check=True)
                                last.then_inc(mm_done, 1)
                    pe.matmul(p_r[:, 0:TH], zero[:, 0, :], zero[:, 1, 0:TH], start=False, stop=True,
                              skip_group_check=True).then_inc(sums_done, 1)
                    pe.wait_ge(scale_ready, 1)
                    pe.transpose(p_rt[0:TH, 0:P], rs[:, :], ident[:, :]).then_inc(turned, 1)

            with ExitStack() as p6:
                JG = Q
                G2 = T // (2 * JG)
                HF1 = H * F1
                JP = 2
                m16 = sb("m16c", [P, 2, JG, CW], BF16, p6)
                uw = sb("uw", [P, H, JG, CW], BF16, p6)
                nrow = sb("nrow", [P, 2, Q, H, P], BF16, p6)
                att = sb("att", [P, 2, H, F], F32, p6)
                rden = sb("rden6", [P, Q, H], F32, p6)
                zero = sb("zero6", [P, P], F16, p6)
                acc = [ps(f"hacc{k}", [P, Q, 512], p6) for k in range(2)]
                row_in = [sem("g_row_in0"), sem("g_row_in1")]
                stored = [sem("g_stored0"), sem("g_stored1")]
                m_done, mv_done, u_done = sem("g_mask_pool"), sem("g_mask_dve"), sem("g_u_done")
                va_done, vd_done = sem("g_weights_act"), sem("g_weights_dve")
                mm_done, chunk_done, att_ready = sem("g_mm_done"), sem("g_chunk_done"), sem("g_att_ready")
                zeroed, steps = sem("g_zeroed"), sem("g_steps")
                OU, OM, OA = 2 * H, H, Q
                block = p6.enter_context(nc.Block())

                @block.sync
                def _(sp):
                    sp.sem_inc(stored[0], 16)
                    sp.sem_inc(stored[1], 16)

                    def rows(c, half):
                        src = row_d[ds(c * Q, Q), :, :].rearrange("t h p -> (t h p)")
                        sp.dma_start(nrow[:, half, :, :, :].rearrange("p t h i -> p (t h i)"),
                                     src.partition_broadcast(P)).then_inc(row_in[half], 16)
                    rows(0, 0)
                    rows(1, 1)

                    def store(c):
                        for it in range(Q):
                            sp.wait_ge(att_ready, OA + c * Q + it + 1)
                            sp.dma_start(att_d[:, ds(c * Q + it, 1), :].rearrange("p a f -> p (a f)"),
                                         att[:, it % 2, :, :].rearrange("p h f -> p (h f)"))\
                                .then_inc(stored[it % 2], 16)

                    if C > 2:
                        with sp.Fori(0, C // 2 - 1) as cp:
                            for half in range(2):
                                store(2 * cp + half)
                                rows(2 * cp + half + 2, half)
                    store(C - 2)
                    store(C - 1)
                    sp.wait_ge(stored[0], 16 + 16 * C * 2)
                    sp.wait_ge(stored[1], 16 + 16 * C * 2)
                    sp.wait_ge(row_in[0], 16 * (C // 2))
                    sp.wait_ge(row_in[1], 16 * (C // 2))

                @block.gpsimd
                def _(pool):
                    pool.memset(zero[:, :], 0.0).then_inc(zeroed, 1)
                    with pool.Fori(0, C) as c:
                        with pool.Fori(0, G2) as r:
                            for u in range(2):
                                n = (c * G2 + r) * 2 + u
                                pool.wait_ge(u_done, OU + (n - 1) * H)
                                pool.tensor_copy(m16[:, u, 0:JP, :],
                                                 mask[:, ds((r * 2 + u) * JG, JP), ds(c * CW, CW)])\
                                    .then_inc(m_done, 1)

                @block.scalar
                def _(act):
                    with act.Fori(0, C) as c:
                        with act.Fori(0, G2) as r:
                            for u in range(2):
                                for k in range(H):
                                    hk = ((c * G2 + r) * 2 + u) * H + k
                                    act.wait_ge(u_done, OU + hk + 1)
                                    act.nop(nofuse=True)
                                    for jt in range(2):
                                        j = (r * 2 + u) * JG + jt
                                        act.activation(uw[:, k, jt, :].bitcast(I16), uw[:, k, jt, :], ACT.Relu,
                                                       bias=kb[:, k, ds(j, 1)]).then_inc(va_done, 1)

                @block.vector
                def _(v):
                    v.sem_inc(u_done, OU)
                    v.sem_inc(att_ready, OA)

                    def unit(c, half, r):
                        for u in range(2):
                            n = (c * G2 + r) * 2 + u
                            v.tensor_copy(m16[:, u, JP:JG, :],
                                          mask[:, ds((r * 2 + u) * JG + JP, JG - JP), ds(c * CW, CW)])\
                                .then_inc(mv_done, 1)
                            v.wait_ge(mv_done, n + 1)
                            v.wait_ge(m_done, n + 1)
                            for k in range(H):
                                hk = n * H + k
                                v.wait_ge(mm_done, OM + hk - H + 1)
                                v.tensor_tensor(uw[:, k, :, :].rearrange("p j (t i) -> p j t i", i=P),
                                                m16[:, u, :, :].rearrange("p j (t i) -> p j t i", i=P),
                                                nrow[:, half, :, k, :].unsqueeze(1).to_broadcast([P, JG, Q, P]),
                                                ALU.mult).then_inc(u_done, 1)
                                v.wait_ge(u_done, OU + hk + 1)
                                for jt in range(2, JG):
                                    j = (r * 2 + u) * JG + jt
                                    v.tensor_scalar(uw[:, k, jt, :].bitcast(I16), uw[:, k, jt, :],
                                                    kb[:, k, ds(j, 1)], 0.0, ALU.add, ALU.max)\
                                        .then_inc(vd_done, 1)

                    def first(c, half, turn):
                        v.wait_ge(row_in[half], 16 * (turn + 1))
                        unit(c, half, 0)

                    def rest(c, half):
                        if G2 > 1:
                            with v.Fori(1, G2) as r:
                                unit(c, half, r)

                    def drain(c, half):
                        a = acc[half][:, :, 0:HF1].rearrange("p i (h f) -> p i h f", f=F1)
                        step = Steps(v, steps, c * 2)
                        v.wait_ge(att_ready, OA + c * Q)
                        v.wait_ge(chunk_done, c + 1)
                        step(v.tensor_scalar(rden[:, :, :], a[:, :, :, F], 1e-36, None, ALU.max))
                        step(v.reciprocal(rden[:, :, :], rden[:, :, :]))
                        for it in range(Q):
                            v.wait_ge(stored[it % 2], 16 + 16 * (2 * c + it // 2))
                            v.tensor_tensor(att[:, it % 2, :, :], a[:, it, :, 0:F],
                                            rden[:, it, :].unsqueeze(2).to_broadcast([P, H, F]),
                                            ALU.mult).then_inc(att_ready, 1)

                    first(0, 0, 0)
                    rest(0, 0)
                    if C > 2:
                        with v.Fori(0, C // 2 - 1) as cp:
                            for half in range(2):
                                c = 2 * cp + half + 1
                                first(c, 1 - half, cp + half)
                                drain(c - 1, half)
                                rest(c, 1 - half)
                    first(C - 1, 1, C // 2 - 1)
                    drain(C - 2, 0)
                    rest(C - 1, 1)
                    drain(C - 1, 1)

                @block.tensor
                def _(pe):
                    pe.sem_inc(mm_done, OM)
                    pe.wait_ge(zeroed, 1)
                    with pe.Fori(0, C // 2) as cp:
                        for half in range(2):
                            c = 2 * cp + half
                            pe.wait_ge(att_ready, OA + (c - 1) * Q)
                            for it in range(Q):
                                for k in range(H):
                                    pe.matmul(acc[half][:, it, k * F1:(k + 1) * F1], zero[:, :],
                                              xh[:, 0, 0, 0, :], start=k == 0, stop=False, skip_group_check=True)
                            with pe.Fori(0, G2) as r:
                                for u in range(2):
                                    for k in range(H):
                                        hk = ((c * G2 + r) * 2 + u) * H + k
                                        for jt in range(JG):
                                            j = (r * 2 + u) * JG + jt
                                            if jt < 2:
                                                pe.wait_ge(va_done, 2 * hk + jt + 1)
                                            else:
                                                pe.wait_ge(vd_done, 2 * hk + jt - 1)
                                            for it in range(Q):
                                                for part in range(2):
                                                    last = pe.matmul(
                                                        acc[half][:, it, k * F1:(k + 1) * F1],
                                                        uw[:, k, jt, it * P:(it + 1) * P],
                                                        xh[:, k, ds(j, 1), part, :].rearrange("p a f -> p (a f)"),
                                                        start=False, stop=False, skip_group_check=True)
                                        last.then_inc(mm_done, 1)
                            for it in range(Q):
                                for k in range(H):
                                    last = pe.matmul(acc[half][:, it, k * F1:(k + 1) * F1], zero[:, :],
                                                     xh[:, 0, 0, 0, :], start=False, stop=k == H - 1,
                                                     skip_group_check=True)
                            last.then_inc(chunk_done, 1)

        mask_scope.close()
        with ExitStack() as p7:
            gw = sb("gw", [P, H, F], F32, p7)
            wt = [sb(f"wt{k}", [P, 3 * F], F32, p7) for k in range(4)]
            bias = sb("bias", [P, 2, 4 * F], F32, p7)
            bhh = sb("bhh", [P, 2, 2 * F], F32, p7)
            sg = sb("sg7", [P, 2, Q, F], F32, p7)
            hg = sb("hg7", [P, 2, Q, F], F32, p7)
            xg = sb("xg7", [P, 2, Q, F], F32, p7)
            ag = sb("ag7", [P, 2, Q, H * F], F32, p7)
            s_t = sb("s_t", [P, CW], F32, p7)
            h_t = sb("h_t", [P, CW], F32, p7)
            a_t = sb("a_t", [P, H, CW], F32, p7)
            n_t = sb("n_t", [P, CW], F32, p7)
            bpart = sb("bpart", [P, 2, 3, 4 * F], BF16, p7)
            brow = sb("brow", [P, 2, 4 * F], BF16, p7)
            ones = sb("ones", [P, P], BF16, p7)
            rz = sb("rz", [P, 2, 2, Q, 2 * F], F32, p7)
            new = sb("new", [P, 2, 2, Q, F], F32, p7)
            cell = sb("cell", [P, 2, Q, F], F32, p7)
            y = sb("y", [P, 2, Q, F], F32, p7)
            p_t = [ps(f"p_t7{k}", [P, CW], p7) for k in range(2)]
            p_s = ps("p_s", [P, CW], p7)
            gates = ps("gates", [P, Q, 4 * F], p7)
            loaded = sem("h_loaded")
            g_in = [sem("h_in0"), sem("h_in1")]
            turned, copied = sem("h_turned"), sem("h_copied")
            gates_done, gates_read = sem("h_gates_done"), sem("h_gates_read")
            ones_ready, bias_ready = sem("h_ones_ready"), sem("h_bias_ready")
            rz_done, n_done = sem("h_rz_done"), sem("h_n_done")
            steps, y_ready = sem("h_steps"), sem("h_y_ready")
            stored = [sem("h_stored0"), sem("h_stored1")]
            block = p7.enter_context(nc.Block())
            parts = [(e_wih_t, e_bih, e_bhh), (n_wih_t, n_bih, n_bhh)]

            @block.sync
            def _(sp):
                sp.dma_start(gw[:, :, :], gat_w.rearrange("h f g -> f h g")).then_inc(loaded, 16)
                for k, weight in enumerate((e_wih_t, e_whh_t, n_wih_t, n_whh_t)):
                    sp.dma_start(wt[k][:, :], weight).then_inc(loaded, 16)
                for k, (bi, bh) in enumerate(((e_bih, e_bhh), (n_bih, n_bhh))):
                    sp.dma_start(bias[:, k, 0:3 * F], bi.partition_broadcast(P)).then_inc(loaded, 16)
                    sp.dma_start(bias[:, k, 3 * F:4 * F], bh[2 * F:3 * F].partition_broadcast(P)).then_inc(loaded, 16)
                    sp.dma_start(bhh[:, k, :], bh[0:2 * F].partition_broadcast(P)).then_inc(loaded, 16)
                sp.sem_inc(stored[0], 16)
                sp.sem_inc(stored[1], 16)

                def load(q, s):
                    for to, of in ((sg, sup_d), (hg, h1_d), (xg, x1_d), (ag, att_d)):
                        sp.dma_start(to[:, s, :, :], of[:, ds(q * Q, Q), :]).then_inc(g_in[s], 16)

                def store(q, s):
                    sp.wait_ge(y_ready, 2 + q + 1)
                    sp.dma_start(out_v[:, ds(q * Q, Q), :], y[:, s, :, :]).then_inc(stored[s], 16)

                load(0, 0)
                load(1, 1)
                if NG > 2:
                    with sp.Fori(0, NG // 2 - 1) as qp:
                        for s in range(2):
                            store(2 * qp + s, s)
                            load(2 * qp + s + 2, s)
                store(NG - 2, 0)
                store(NG - 1, 1)
                sp.wait_ge(stored[0], 16 + 16 * (NG // 2))
                sp.wait_ge(stored[1], 16 + 16 * (NG // 2))

            @block.gpsimd
            def _(pool):
                pool.memset(ones[:, :], 1.0).then_inc(ones_ready, 1)

            @block.tensor
            def _(pe):
                def turn(q, n, bank, of):
                    pe.wait_ge(copied, 1 + 6 * q + max(n - 1, 0))
                    for k in range(Q):
                        last = pe.transpose(p_t[bank][:, k * P:(k + 1) * P], of(k), ident[:, :])
                    last.then_inc(turned, 1)

                def cell_gates(x_t, wi, wh, g):
                    for k in range(Q):
                        pe.matmul(gates[:, k, :], ones[:, :], brow[:, g, :], start=True, stop=False,
                                  skip_group_check=True)
                        t, h = x_t[:, k * P:(k + 1) * P], h_t[:, k * P:(k + 1) * P]
                        pe.matmul(gates[:, k, 0:2 * F], t, wi[:, 0:2 * F], start=False, stop=False,
                                  skip_group_check=True)
                        pe.matmul(gates[:, k, 0:2 * F], h, wh[:, 0:2 * F], start=False, stop=False,
                                  skip_group_check=True)
                        pe.matmul(gates[:, k, 2 * F:3 * F], t, wi[:, 2 * F:3 * F], start=False, stop=False,
                                  skip_group_check=True)
                        last = pe.matmul(gates[:, k, 3 * F:4 * F], h, wh[:, 2 * F:3 * F], start=False, stop=True,
                                         skip_group_check=True)
                    last.then_inc(gates_done, 1)

                pe.sem_inc(gates_done, 1)
                pe.wait_ge(loaded, 16 * 11)
                pe.wait_ge(ones_ready, 1)
                pe.wait_ge(bias_ready, 1)
                with pe.Fori(0, NG // 2) as qp:
                    for s in range(2):
                        q = 2 * qp + s
                        pe.wait_ge(g_in[s], 64 * (qp + 1))
                        turn(q, 0, 0, lambda k: sg[:, s, k, :])
                        turn(q, 1, 1, lambda k: hg[:, s, k, :])
                        for h in range(H):
                            turn(q, 2 + h, h % 2, lambda k: ag[:, s, k, h * F:(h + 1) * F])
                        pe.wait_ge(copied, 1 + 6 * q + 2)
                        pe.wait_ge(gates_read, 1 + 2 * q)
                        cell_gates(s_t, wt[0], wt[1], 0)
                        pe.wait_ge(copied, 1 + 6 * q + 5)
                        for h in range(H):
                            last = pe.matmul(p_s[:, :], gw[:, h, :], a_t[:, h, :], start=h == 0, stop=h == H - 1)
                        last.then_inc(turned, 1)
                        pe.wait_ge(copied, 1 + 6 * q + 6)
                        pe.wait_ge(gates_read, 1 + 2 * q + 1)
                        cell_gates(n_t, wt[2], wt[3], 1)

            @block.scalar
            def _(act):
                act.sem_inc(copied, 1)
                with act.Fori(0, NG // 2) as qp:
                    for s in range(2):
                        q = 2 * qp + s
                        def copy(n, to, of, scale=1.0):
                            act.wait_ge(turned, 6 * q + n + 1)
                            act.nop(nofuse=True)
                            act.activation(to, of, ACT.Copy, scale=scale).then_inc(copied, 1)

                        act.wait_ge(gates_done, 1 + 2 * q)
                        act.nop(nofuse=True)
                        copy(0, s_t[:, :], p_t[0][:, :])
                        copy(1, h_t[:, :], p_t[1][:, :])
                        for h in range(H):
                            copy(2 + h, a_t[:, h, :], p_t[h % 2][:, :])
                        act.wait_ge(y_ready, 2 + q - 1)
                        for g in range(2):
                            if g == 0:
                                copy(5, n_t[:, :], p_s[:, :], 1.0 / H)
                            act.wait_ge(gates_done, 1 + 2 * q + g + 1)
                            act.activation(rz[:, s, g, :, :], gates[:, :, 0:2 * F], ACT.Tanh, scale=0.5)\
                               .then_inc(rz_done, 1)
                            act.wait_ge(gates_read, 1 + 2 * q + g + 1)
                            act.activation(new[:, s, g, :, :], new[:, s, g, :, :], ACT.Tanh).then_inc(n_done, 1)

            @block.vector
            def _(v):
                v.sem_inc(y_ready, 2)
                v.sem_inc(gates_read, 1)
                step = Steps(v, steps)
                v.wait_ge(loaded, 16 * 11)
                step(v.tensor_tensor(bias[:, :, 0:2 * F], bias[:, :, 0:2 * F], bhh[:, :, :], ALU.add))
                for part in range(3):
                    step(v.tensor_copy(bpart[:, :, part, :], bias[:, :, :]))
                    if part < 2:
                        step(v.tensor_tensor(bias[:, :, :], bias[:, :, :], bpart[:, :, part, :], ALU.subtract))
                step(v.tensor_scalar(brow[:, :, :], bpart[:, :, 0, :], ident[:, 0:1], None, ALU.mult))
                step(v.scalar_tensor_tensor(brow[:, :, :], bpart[:, :, 1, :], ident[:, 1:2], brow[:, :, :],
                                            ALU.mult, ALU.add))
                v.scalar_tensor_tensor(brow[:, :, :], bpart[:, :, 2, :], ident[:, 2:3], brow[:, :, :],
                                       ALU.mult, ALU.add).then_inc(bias_ready, 1)
                before, per_group = step.n, 12
                with v.Fori(0, NG // 2) as qp:
                    for s in range(2):
                        q = 2 * qp + s
                        step = Steps(v, steps, before + per_group * q)
                        v.wait_ge(g_in[s], 64 * (qp + 1))
                        v.wait_ge(y_ready, 2 + q)
                        for g in range(2):
                            r = rz[:, s, g, :, 0:F]
                            v.wait_ge(rz_done, 2 * q + g + 1)
                            step(v.tensor_scalar(rz[:, s, g, :, :], rz[:, s, g, :, :], 0.5, 0.5, ALU.mult, ALU.add))
                            step(v.tensor_tensor(new[:, s, g, :, :], gates[:, :, 3 * F:4 * F], r, ALU.mult))
                            v.tensor_tensor(new[:, s, g, :, :], gates[:, :, 2 * F:3 * F], new[:, s, g, :, :],
                                            ALU.add).then_inc(gates_read, 1)
                        for g in range(2):
                            z = rz[:, s, g, :, F:2 * F]
                            v.wait_ge(n_done, 2 * q + g + 1)
                            step(v.tensor_tensor(cell[:, g, :, :], hg[:, s, :, :], new[:, s, g, :, :], ALU.subtract))
                            step(v.tensor_tensor(cell[:, g, :, :], cell[:, g, :, :], z, ALU.mult))
                            step(v.tensor_tensor(cell[:, g, :, :], cell[:, g, :, :], new[:, s, g, :, :], ALU.add))
                        step(v.tensor_tensor(cell[:, 0, :, :], cell[:, 0, :, :], cell[:, 1, :, :], ALU.add))
                        step(v.tensor_tensor(cell[:, 0, :, :], cell[:, 0, :, :],
                                             dn[:, ds(q * Q, Q)].unsqueeze(2).to_broadcast([P, Q, F]), ALU.mult))
                        v.wait_ge(stored[s], 16 + 16 * qp)
                        v.tensor_tensor(y[:, s, :, :], cell[:, 0, :, :], xg[:, s, :, :], ALU.add)\
                            .then_inc(y_ready, 1)
                        assert step.n == per_group


def kernel(x, adj, L0_gnn_W, L0_gnn_attn_src, L0_gnn_attn_dst, L1_gnn_gat_W, L1_gnn_gat_a,
           L1_gnn_edge_Wih, L1_gnn_edge_Whh, L1_gnn_edge_bih, L1_gnn_edge_bhh,
           L1_gnn_node_Wih, L1_gnn_node_Whh, L1_gnn_node_bih, L1_gnn_node_bhh):
    import numpy as _np
    import concourse.bacc as _bacc
    from concourse import mybir as _mybir
    from concourse.bass_utils import run_bass_kernel_spmd as _run

    t = lambda a: _np.ascontiguousarray(_np.asarray(a).T)
    c = lambda a: _np.ascontiguousarray(_np.asarray(a))
    gw = c(L1_gnn_gat_W)
    arrays = {
        "x": c(x), "adj_t": t(adj), "w0": c(L0_gnn_W), "w0_t": t(L0_gnn_W),
        "att_src": c(L0_gnn_attn_src), "att_dst": c(L0_gnn_attn_dst),
        "gat_w": gw, "gat_w_t": _np.ascontiguousarray(gw.transpose(0, 2, 1)), "gat_a": c(L1_gnn_gat_a),
        "e_wih_t": t(L1_gnn_edge_Wih), "e_whh_t": t(L1_gnn_edge_Whh),
        "e_bih": c(L1_gnn_edge_bih), "e_bhh": c(L1_gnn_edge_bhh),
        "n_wih_t": t(L1_gnn_node_Wih), "n_whh_t": t(L1_gnn_node_Whh),
        "n_bih": c(L1_gnn_node_bih), "n_bhh": c(L1_gnn_node_bhh),
    }
    nc = _bacc.Bacc("TRN2", target_bir_lowering=False, num_devices=1)
    args = {n: nc.dram_tensor(f"in_{n}", a.shape, _mybir.dt.from_np(a.dtype), kind="ExternalInput").ap()
            for n, a in arrays.items()}
    out = nc.dram_tensor("out_x", arrays["x"].shape, _mybir.dt.float32, kind="ExternalOutput").ap()
    graph_layers(nc, out=out, **args)
    r = _run(nc, [{f"in_{n}": a for n, a in arrays.items()}], core_ids=[0])
    return r.results[0]["out_x"]
```

```python
import concourse.bass as bass
from concourse import mybir
from contextlib import ExitStack

F32, F16, BF16 = mybir.dt.float32, mybir.dt.float16, mybir.dt.bfloat16
I16, I32, U8 = mybir.dt.int16, mybir.dt.int32, mybir.dt.uint8
ALU = mybir.AluOpType
ACT = mybir.ActivationFunctionType
AX = mybir.AxisListType
ds = bass.ds


class Steps:

    def __init__(self, eng, sem, base=0):
        self.eng, self.sem, self.base, self.n = eng, sem, base, 0

    def __call__(self, instruction):
        self.n += 1
        instruction.then_inc(self.sem, 1)
        self.eng.wait_ge(self.sem, self.base + self.n)


def graph_layers(nc, x, adj_t, w0, w0_t, att_src, att_dst, gat_w, gat_w_t, gat_a,
                 e_wih_t, e_whh_t, e_bih, e_bhh, n_wih_t, n_whh_t, n_bih, n_bhh, out):
    P = 128
    N, F = x.shape
    T = N // P
    H = gat_w.shape[0]
    Q = 4
    NG = T // Q
    CW = Q * P
    C = N // CW
    F1 = F + 1
    SPLIT = 2048.0
    LOG2E = 1.4426950408889634
    LN2_HI = 0.693359375
    LN2_LO = -2.12194440e-4
    ROUND = 12582912.0
    EPS_LN = 1e-5
    assert F == P and T % (2 * Q) == 0

    x_v = x.rearrange("(t p) f -> p t f", p=P)
    out_v = out.rearrange("(t p) f -> p t f", p=P)
    adj_v = adj_t.rearrange("(t p) i -> p t i", p=P)
    x1_d = nc.dram_tensor("x1_d", (N, F), F32).ap().rearrange("(t p) f -> p t f", p=P)
    h1_d = nc.dram_tensor("h1_d", (N, F), F32).ap().rearrange("(t p) f -> p t f", p=P)
    sup_d = nc.dram_tensor("sup_d", (F, N), F32).ap()
    att_d = nc.dram_tensor("att_d", (N, H * F), F32).ap().rearrange("(t p) f -> p t f", p=P)
    row_d = nc.dram_tensor("row_d", (T, H, P), BF16).ap()

    main = ExitStack()
    with main:
        def sem(name):
            return main.enter_context(nc.semaphore(name))

        def sb(name, shape, dt, ctx=main):
            return ctx.enter_context(nc.sbuf_tensor(name, shape, dt))

        def ps(name, shape, ctx, dt=F32):
            return ctx.enter_context(nc.psum_tensor(name, shape, dt))

        ident = sb("ident", [P, P], F32)

        def run_chunks(eng, first, rest, drain):
            first(0, 0)
            rest(0, 0)
            if C > 2:
                with eng.Fori(0, C // 2 - 1) as cp:
                    for s in range(2):
                        c = 2 * cp + s + 1
                        first(c, 1 - s)
                        drain(c - 1, s)
                        rest(c, 1 - s)
            first(C - 1, 1)
            drain(C - 2, 0)
            rest(C - 1, 1)
            drain(C - 1, 1)

        def pipelined(eng, first, second):
            first(0, 0)
            if NG > 2:
                with eng.Fori(0, NG // 2 - 1) as qp:
                    for s in range(2):
                        first(2 * qp + s + 1, 1 - s)
                        second(2 * qp + s, s)
            first(NG - 1, 1)
            second(NG - 2, 0)
            second(NG - 1, 1)

        def row_stats(v, xs, stats, lo, hi, counted):
            with v.Fori(lo, hi) as q:
                for k in range(Q):
                    v.bn_stats(stats[:, ds(q * Q + k, 1), :].rearrange("p a s -> p (a s)"),
                               xs[:, ds(q * Q + k, 1), :].rearrange("p a f -> p (a f)")).then_inc(counted, 1)

        def mean_and_var(v, step, stats, mean, var, tmp):
            even, odd = (stats[:, :, k:k + 3] for k in (0, 3))
            step(v.tensor_tensor(mean, even[:, :, 1], odd[:, :, 1], ALU.add))
            step(v.tensor_scalar(mean, mean, 0.5, None, ALU.mult))
            step(v.tensor_tensor(tmp, even[:, :, 1], odd[:, :, 1], ALU.subtract))
            step(v.scalar_tensor_tensor(tmp, tmp, 0.25, tmp, ALU.mult, ALU.mult))
            step(v.tensor_tensor(var, even[:, :, 2], odd[:, :, 2], ALU.add))
            step(v.scalar_tensor_tensor(var, var, 1.0 / F, tmp, ALU.mult, ALU.add))

        def inverse_root(v, step, var, std, rstd, var_ready, root_ready):
            v.tensor_scalar(var, var, EPS_LN, None, ALU.add).then_inc(var_ready, 1)
            v.wait_ge(root_ready, 1)
            v.wait_ge(var_ready, 1)
            step(v.reciprocal(rstd, std))
            step(v.tensor_tensor(rstd, rstd, var, ALU.mult))
            step(v.tensor_tensor(std, std, rstd, ALU.add))
            step(v.tensor_scalar(std, std, 0.5, None, ALU.mult))
            step(v.reciprocal(rstd, std))

        dn = sb("dn", [P, T], F32)
        kb = sb("kb", [P, H, T], F32)
        g_all = sb("g_all", [P, H, T], F32)
        pw = sb("pw", [P, T, H], BF16)
        mask_scope = ExitStack()
        main.enter_context(mask_scope)
        mask = sb("mask", [P, T, N], U8, mask_scope)

        o0_scope = ExitStack()
        main.enter_context(o0_scope)
        o0 = sb("o0", [P, T, F], F32, o0_scope)

        with ExitStack() as l0:
            hx = sb("hx", [P, T, F1], F32, l0)
            scal = sb("scal", [P, 8, T], F32, l0)
            a_src, a_dst, es, es2, nes, eps, t0, t1 = (scal[:, k, :] for k in range(8))
            rrow = sb("rrow", [P, N], F32, l0)

            with ExitStack() as p0:
                xs = o0
                stats = sb("stats", [P, T, 6], F32, p0)
                mv = sb("mv", [P, T, 2], F32, p0)
                mean, var = mv[:, :, 0], mv[:, :, 1]
                st = sb("st", [P, 2, T], F32, p0)
                std, rstd = st[:, 0, :], st[:, 1, :]
                w0_s = sb("w0_s", [P, F], F32, p0)
                w0t_s = sb("w0t_s", [P, F], F32, p0)
                att_s = sb("att_s", [P, 2], F32, p0)
                u_s = sb("u_s", [P, 2], F32, p0)
                udst = sb("udst", [P, P], F32, p0)
                h0 = sb("h0", [P, 2, Q, F], F32, p0)
                h0t = sb("h0t", [P, 2, CW], F32, p0)
                amax = sb("amax", [P, 2], F32, p0)
                p_t = ps("p_t", [P, 2, CW], p0)
                p_h = ps("p_h", [P, 2, Q, F], p0)
                p_ad = ps("p_ad", [P, 2, 512], p0)
                p_d = ps("p_d", [P, 2, CW], p0)
                loaded, steps = sem("a_loaded"), sem("a_steps")
                x_in = [sem("a_x_in0"), sem("a_x_in1")]
                var_ready, root_ready = sem("a_var_ready"), sem("a_root_ready")
                counted, scaled = sem("a_counted"), sem("a_scaled")
                id_ready, u_ready, u_copied = sem("a_id"), sem("a_u_ready"), sem("a_u_copied")
                h0_ready, h0_turned = sem("a_h0_ready"), sem("a_h0_turned")
                h0t_ready, h_done = sem("a_h0t_ready"), sem("a_h_done")
                h_copied, d_copied = sem("a_h_copied"), sem("a_d_copied")
                rowmax, allmax = sem("a_rowmax"), sem("a_allmax")
                exp_in, exp_out = sem("a_exp_in"), sem("a_exp_out")
                block = p0.enter_context(nc.Block())

                @block.sync
                def _(sp):
                    sp.dma_start(w0_s[:, :], w0).then_inc(loaded, 16)
                    sp.dma_start(w0t_s[:, :], w0_t).then_inc(loaded, 16)
                    sp.dma_start(att_s[:, 0:1], att_src.rearrange("a f -> f a")).then_inc(loaded, 16)
                    sp.dma_start(att_s[:, 1:2], att_dst.rearrange("a f -> f a")).then_inc(loaded, 16)
                    for half in range(2):
                        rows = slice(half * T // 2, (half + 1) * T // 2)
                        sp.dma_start(xs[:, rows, :], x_v[:, rows, :]).then_inc(x_in[half], 16)

                @block.gpsimd
                def _(pool):
                    pool.memset(ident[:, :], 0.0).then_inc(id_ready, 1)
                    pool.wait_ge(id_ready, 1)
                    pool.affine_select(out=ident[:, :], in_=ident[:, :], compare_op=ALU.not_equal, fill=1.0,
                                       base=0, pattern=[[-1, P]], channel_multiplier=1).then_inc(id_ready, 1)
                    pool.wait_ge(rowmax, 1)
                    pool.partition_all_reduce(amax[:, 1:2], amax[:, 0:1], P,
                                              bass.bass_isa.ReduceOp.max).then_inc(allmax, 1)

                @block.tensor
                def _(pe):
                    pe.sem_inc(h0_turned, 2)
                    pe.sem_inc(h_done, 2)
                    pe.wait_ge(loaded, 64)
                    pe.matmul(p_ad[:, 0, 0:2], w0_s[:, :], att_s[:, :], start=True, stop=True).then_inc(u_ready, 1)
                    pe.wait_ge(id_ready, 2)
                    pe.wait_ge(u_copied, 2)

                    def turn(q, s):
                        pe.wait_ge(h0_ready, q + 1)
                        pe.wait_ge(h0t_ready, 2 + q - 1)
                        for k in range(Q):
                            last = pe.transpose(p_t[:, s, k * P:(k + 1) * P], h0[:, s, k, :], ident[:, :])
                        last.then_inc(h0_turned, 1)

                    def products(q, s):
                        pe.wait_ge(h0t_ready, 2 + q + 1)
                        pe.wait_ge(h_copied, 2 + q - 1)
                        pe.wait_ge(d_copied, 2 + q - 1)
                        for k in range(Q):
                            t = h0t[:, s, k * P:(k + 1) * P]
                            pe.matmul(p_h[:, s, k, :], t, w0t_s[:, :], start=True, stop=True)
                            pe.matmul(p_ad[:, s, 2 * k:2 * k + 2], t, u_s[:, :], start=True, stop=True)
                        pe.matmul(p_d[:, s, :], udst[:, :], h0t[:, s, :], start=True, stop=True)\
                            .then_inc(h_done, 1)

                    pipelined(pe, turn, products)

                @block.scalar
                def _(act):
                    act.sem_inc(h0t_ready, 2)
                    act.sem_inc(d_copied, 2)
                    act.wait_ge(var_ready, 1)
                    act.activation(std, var, ACT.Sqrt).then_inc(root_ready, 1)

                    def turned(q, s):
                        act.wait_ge(h0_turned, 2 + q + 1)
                        act.nop(nofuse=True)
                        act.wait_ge(h_done, 2 + q - 1)
                        act.nop(nofuse=True)
                        act.activation(h0t[:, s, :], p_t[:, s, :], ACT.Copy).then_inc(h0t_ready, 1)

                    def dst_row(q, s):
                        act.wait_ge(h_done, 2 + q + 1)
                        act.nop(nofuse=True)
                        act.activation(rrow[:, ds(q * CW, CW)], p_d[:, s, :], ACT.Copy).then_inc(d_copied, 1)

                    pipelined(act, turned, dst_row)
                    act.wait_ge(exp_in, 1)
                    act.activation(es, t0, ACT.Exp).then_inc(exp_out, 1)
                    act.activation(es2, t0, ACT.Exp, scale=0.2).then_inc(exp_out, 1)
                    act.wait_ge(exp_in, 2)
                    act.activation(eps, t1, ACT.Exp).then_inc(exp_out, 1)
                    act.wait_ge(exp_in, 3)
                    act.activation(rrow[:, :], rrow[:, :], ACT.Exp).then_inc(exp_out, 1)

                @block.vector
                def _(v):
                    step = Steps(v, steps)
                    v.sem_inc(h_copied, 2)
                    v.wait_ge(u_ready, 1)
                    v.tensor_copy(u_s[:, :], p_ad[:, 0, 0:2]).then_inc(u_copied, 1)
                    v.wait_ge(u_copied, 1)
                    v.tensor_copy(udst[:, :], u_s[:, 1:2].to_broadcast([P, P])).then_inc(u_copied, 1)
                    for half in range(2):
                        v.wait_ge(x_in[half], 16)
                        row_stats(v, xs, stats, half * NG // 2, (half + 1) * NG // 2, counted)
                    v.wait_ge(counted, T)
                    mean_and_var(v, step, stats, mean, var, std)
                    inverse_root(v, step, var, std, rstd, var_ready, root_ready)

                    def norm(q, s):
                        v.wait_ge(h0_turned, 2 + q - 1)
                        for k in range(Q):
                            t = ds(q * Q + k, 1)
                            v.tensor_scalar(h0[:, s, k, :], xs[:, t, :].rearrange("p a f -> p (a f)"),
                                            mean[:, t], rstd[:, t], ALU.subtract, ALU.mult).then_inc(scaled, 1)
                        v.wait_ge(scaled, (q + 1) * Q)
                        v.tensor_scalar(h0[:, s, :, :], h0[:, s, :, :], 0.0, None, ALU.max).then_inc(h0_ready, 1)

                    def keep(q, s):
                        v.wait_ge(h_done, 2 + q + 1)
                        v.tensor_copy(hx[:, ds(q * Q, Q), 0:F], p_h[:, s, :, :])
                        pair = p_ad[:, s, 0:2 * Q].rearrange("p (k two) -> p k two", two=2)
                        v.tensor_copy(a_src[:, ds(q * Q, Q)], pair[:, :, 0])
                        v.tensor_copy(a_dst[:, ds(q * Q, Q)], pair[:, :, 1]).then_inc(h_copied, 1)

                    norm(0, 0)
                    norm(1, 1)
                    if NG > 2:
                        with v.Fori(0, NG // 2 - 1) as qp:
                            for s in range(2):
                                norm(2 * qp + s + 2, s)
                                keep(2 * qp + s, s)
                    keep(NG - 2, 0)
                    keep(NG - 1, 1)
                    v.wait_ge(h_copied, 2 + NG)
                    step(v.memset(hx[:, :, F:F1], 1.0))
                    v.tensor_reduce(amax[:, 0:1], a_src, AX.X, ALU.max).then_inc(rowmax, 1)
                    v.wait_ge(allmax, 1)
                    v.tensor_scalar(t0, a_src, amax[:, 1:2], None, ALU.subtract).then_inc(exp_in, 1)
                    step(v.tensor_scalar(a_dst, a_dst, amax[:, 1:2], None, ALU.add))
                    step(v.tensor_scalar(t1, a_dst, 0.8, 80.0, ALU.mult, ALU.add))
                    step(v.tensor_scalar(t1, t1, 0.0, None, ALU.min))
                    v.tensor_tensor(t1, t1, a_dst, ALU.subtract).then_inc(exp_in, 1)
                    v.wait_ge(d_copied, 2 + NG)
                    step(v.tensor_scalar(rrow[:, :], rrow[:, :], amax[:, 1:2], -0.8, ALU.add, ALU.mult))
                    v.tensor_scalar(rrow[:, :], rrow[:, :], 80.0, None, ALU.min).then_inc(exp_in, 1)
                    v.wait_ge(exp_out, 1)
                    step(v.tensor_scalar(nes, es, -1.0, None, ALU.mult))
                    v.wait_ge(exp_out, 3)
                    step(v.tensor_scalar(eps, eps, 1e-8, None, ALU.mult))

            with ExitStack() as p1:
                JG, SL = 2, 4
                G4 = T // (JG * SL)
                OFF = 8
                adj = sb("adj", [P, SL, JG, CW], F32, p1)
                rel = sb("rel", [P, 2, CW], F32, p1)
                w = sb("w", [P, 4, CW], F32, p1)
                rden = sb("rden", [P, 2, Q], F32, p1)
                zero = sb("zero", [P, 2, P], BF16, p1)
                acc = [ps(f"acc{k}", [P, Q, 512], p1) for k in range(2)]
                adj_in = [sem(f"b_adj_in{k}") for k in range(SL)]
                rel_done, w_done = sem("b_rel_done"), sem("b_w_done")
                mask_done = [sem(f"b_mask_done{u}") for u in range(SL)]
                mask_act, mm_done = sem("b_mask_act"), sem("b_mm_done")
                UA = 2
                chunk_done, drained = sem("b_chunk_done"), sem("b_drained")
                steps, zeroed = sem("b_steps"), sem("b_zeroed")
                block = p1.enter_context(nc.Block())

                @block.sync
                def _(sp):
                    with sp.Fori(0, C) as c:
                        with sp.Fori(0, G4) as r:
                            for u in range(SL):
                                n = (c * G4 + r) * SL + u
                                used = sp.snap(OFF + JG * (n - SL + 1))
                                kept = sp.snap(OFF + c * G4 + r)
                                sp.wait_ge(w_done, used)
                                sp.nop(nofuse=True)
                                sp.wait_ge(mask_act if u == UA else mask_done[u], kept)
                                sp.dma_start(adj[:, u, :, :],
                                             adj_v[:, ds((r * SL + u) * JG, JG), ds(c * CW, CW)])\
                                    .then_inc(adj_in[u], 16)

                @block.gpsimd
                def _(pool):
                    pool.memset(zero[:, :, :], 0.0).then_inc(zeroed, 1)
                    for u in range(SL):
                        pool.sem_inc(mask_done[u], OFF)
                    with pool.Fori(0, C) as c:
                        with pool.Fori(0, G4) as r:
                            for u in range(SL):
                                if u != UA:
                                    pool.wait_ge(adj_in[u], 16 * (c * G4 + r + 1))
                                    pool.tensor_copy(mask[:, ds((r * SL + u) * JG, 1), ds(c * CW, CW)],
                                                     adj[:, u, 0:1, :]).then_inc(mask_done[u], 1)

                @block.scalar
                def _(act):
                    act.sem_inc(rel_done, OFF)
                    act.sem_inc(mask_act, OFF)
                    with act.Fori(0, C) as c:
                        with act.Fori(0, G4) as r:
                            for u in range(SL):
                                for jt in range(JG):
                                    k = ((c * G4 + r) * SL + u) * JG + jt
                                    j = (r * SL + u) * JG + jt
                                    act.wait_ge(w_done, OFF + k - 1)
                                    act.nop(nofuse=True)
                                    act.activation(rel[:, jt, :], rrow[:, ds(c * CW, CW)], ACT.Relu,
                                                   bias=nes[:, ds(j, 1)], scale=es2[:, ds(j, 1)])\
                                       .then_inc(rel_done, 1)
                                if u == UA:
                                    act.wait_ge(adj_in[u], 16 * (c * G4 + r + 1))
                                    act.nop(nofuse=True)
                                    act.activation(mask[:, ds((r * SL + u) * JG, JG), ds(c * CW, CW)],
                                                   adj[:, u, :, :], ACT.Copy).then_inc(mask_act, 1)

                @block.vector
                def _(v):
                    v.sem_inc(w_done, OFF)
                    v.sem_inc(drained, 2)

                    def weights(c, r):
                        for u in range(SL):
                            v.wait_ge(adj_in[u], 16 * (c * G4 + r + 1))
                            if u != UA:
                                v.tensor_copy(mask[:, ds((r * SL + u) * JG + 1, JG - 1), ds(c * CW, CW)],
                                              adj[:, u, 1:JG, :])
                            for jt in range(JG):
                                k = ((c * G4 + r) * SL + u) * JG + jt
                                j = (r * SL + u) * JG + jt
                                v.wait_ge(rel_done, OFF + k + 1)
                                v.wait_ge(mm_done, OFF + k - 3)
                                v.scalar_tensor_tensor(w[:, (u * JG + jt) % 4, :], rel[:, jt, :],
                                                       es[:, ds(j, 1)], adj[:, u, jt, :],
                                                       ALU.add, ALU.mult).then_inc(w_done, 1)

                    def rest(c, half):
                        if G4 > 1:
                            with v.Fori(1, G4) as r:
                                weights(c, r)

                    def drain(c, half):
                        a = acc[half]
                        step = Steps(v, steps, c * 2)
                        v.wait_ge(drained, 2 + c)
                        v.wait_ge(chunk_done, c + 1)
                        step(v.tensor_tensor(rden[:, 0, :], a[:, :, F], eps[:, ds(c * Q, Q)], ALU.add))
                        step(v.reciprocal(rden[:, 1, :], rden[:, 0, :]))
                        v.tensor_tensor(o0[:, ds(c * Q, Q), :], a[:, :, 0:F],
                                        rden[:, 1, :].unsqueeze(2).to_broadcast([P, Q, F]),
                                        ALU.mult).then_inc(drained, 1)

                    run_chunks(v, lambda c, half: weights(c, 0), rest, drain)

                @block.tensor
                def _(pe):
                    pe.sem_inc(mm_done, OFF)
                    pe.wait_ge(zeroed, 1)
                    with pe.Fori(0, C // 2) as cp:
                        for half in range(2):
                            c = 2 * cp + half
                            pe.wait_ge(drained, 2 + c - 1)
                            for it in range(Q):
                                pe.matmul(acc[half][:, it, 0:P], zero[:, 0, :], zero[:, 1, :],
                                          start=True, stop=False, skip_group_check=True)
                                pe.matmul(acc[half][:, it, P:P + 1], zero[:, 0, :], zero[:, 1, 0:1],
                                          start=False, stop=False, skip_group_check=True)
                            with pe.Fori(0, G4) as r:
                                for u in range(SL):
                                    for jt in range(JG):
                                        k = ((c * G4 + r) * SL + u) * JG + jt
                                        j = (r * SL + u) * JG + jt
                                        pe.wait_ge(w_done, OFF + k + 1)
                                        for it in range(Q):
                                            last = pe.matmul(acc[half][:, it, 0:F1],
                                                             w[:, (u * JG + jt) % 4, it * P:(it + 1) * P],
                                                             hx[:, ds(j, 1), :].rearrange("p a f -> p (a f)"),
                                                             start=False, stop=False, skip_group_check=True)
                                        last.then_inc(mm_done, 1)
                            for it in range(Q):
                                last = pe.matmul(acc[half][:, it, 0:P], zero[:, 0, :], zero[:, 1, :],
                                                 start=False, stop=True, skip_group_check=True)
                            last.then_inc(chunk_done, 1)

        with ExitStack() as l1a:
            h2 = sb("h2", [P, T, 2, F], F16, l1a)
            xs = sb("xs2", [P, T, F], F32, l1a)
            mv = sb("mv2", [P, T, 2], F32, l1a)
            mean, var = mv[:, :, 0], mv[:, :, 1]
            rstd = sb("rstd2", [P, T], F32, l1a)
            wa = sb("wa", [P, H], F32, l1a)
            with ExitStack() as p2:
                HT = T // 2
                ex = h2[:, :, :, :].rearrange("p t s f -> p (t s f)").bitcast(F32)\
                    .rearrange("p (t f) -> p t f", f=F)
                stats = sb("stats2", [P, T, 6], F32, p2)
                std = sb("std2", [P, T], F32, p2)
                off = sb("off", [P, P], BF16, p2)
                gwt = sb("gwt", [P, H, F], F32, p2)
                ga = sb("ga", [P, H], F32, p2)
                p_wa = ps("p_wa", [P, 512], p2)
                x_in = [sem("c_x_in0"), sem("c_x_in1")]
                steps, counted = sem("c_steps"), sem("c_counted")
                weights_in, wa_done = sem("c_weights_in"), sem("c_wa_done")
                var_ready, root_ready = sem("c_var_ready"), sem("c_root_ready")
                neg_ready, exp_ready = sem("c_neg_ready"), sem("c_exp_ready")
                x1_ready, stored = sem("c_x1_ready"), sem("c_stored")
                off_ready, cleared = sem("c_off_ready"), sem("c_cleared")
                block = p2.enter_context(nc.Block())

                @block.sync
                def _(sp):
                    for half in range(2):
                        rows = slice(half * HT, (half + 1) * HT)
                        sp.dma_start(xs[:, rows, :], x_v[:, rows, :]).then_inc(x_in[half], 16)
                    sp.dma_start(gwt[:, :, :], gat_w_t.rearrange("h g f -> g h f")).then_inc(weights_in, 16)
                    with nc.allow_non_contiguous_dma(reason="three short vectors"):
                        sp.dma_start(ga[:, :], gat_a[:, 0:F, 0].rearrange("h f -> f h")).then_inc(weights_in, 16)
                    for half in range(2):
                        sp.wait_ge(x1_ready, half + 1)
                        rows = slice(half * HT, (half + 1) * HT)
                        sp.dma_start(x1_d[:, rows, :], xs[:, rows, :]).then_inc(stored, 16)
                    sp.wait_ge(stored, 32)

                @block.gpsimd
                def _(pool):
                    pool.memset(off[:, :], 1.0).then_inc(off_ready, 1)
                    pool.wait_ge(off_ready, 1)
                    pool.affine_select(out=off[:, :], in_=off[:, :], compare_op=ALU.not_equal, fill=0.0,
                                       base=0, pattern=[[-1, P]], channel_multiplier=1).then_inc(off_ready, 1)

                @block.tensor
                def _(pe):
                    pe.wait_ge(weights_in, 32)
                    for k in range(H):
                        last = pe.matmul(p_wa[:, k:k + 1], gwt[:, k, :], ga[:, k:k + 1], start=True, stop=True)
                    last.then_inc(wa_done, 1)

                @block.scalar
                def _(act):
                    for half in range(2):
                        rows = slice(half * HT, (half + 1) * HT)
                        act.wait_ge(neg_ready, half + 1)
                        act.activation(ex[:, rows, :], ex[:, rows, :], ACT.Exp).then_inc(exp_ready, 1)
                    act.wait_ge(var_ready, 1)
                    act.activation(std[:, :], var, ACT.Sqrt).then_inc(root_ready, 1)

                @block.vector
                def _(v):
                    step = Steps(v, steps)
                    for half in range(2):
                        rows = slice(half * HT, (half + 1) * HT)
                        v.tensor_scalar(ex[:, rows, :], o0[:, rows, :], 0.0, None, ALU.min).then_inc(neg_ready, 1)
                    whole = mask[:, :, :]
                    blocks = bass.AP(tensor=whole.tensor, offset=whole.offset,
                                     ap=[whole.ap[0], [N + P, T], [1, P]])
                    v.wait_ge(off_ready, 2)
                    v.tensor_tensor(blocks, blocks, off[:, :].unsqueeze(1).to_broadcast([P, T, P]),
                                    ALU.mult).then_inc(cleared, 1)
                    for half in range(2):
                        rows = slice(half * HT, (half + 1) * HT)
                        v.wait_ge(x_in[half], 16)
                        v.wait_ge(exp_ready, half + 1)
                        step(v.scalar_tensor_tensor(ex[:, rows, :], o0[:, rows, :], 0.0, ex[:, rows, :],
                                                    ALU.max, ALU.add))
                        v.scalar_tensor_tensor(xs[:, rows, :], ex[:, rows, :], -1.0, xs[:, rows, :],
                                               ALU.add, ALU.add).then_inc(x1_ready, 1)
                        v.wait_ge(x1_ready, half + 1)
                        row_stats(v, xs, stats, half * NG // 2, (half + 1) * NG // 2, counted)
                    v.wait_ge(counted, T)
                    mean_and_var(v, step, stats, mean, var, std[:, :])
                    v.wait_ge(cleared, 1)
                    inverse_root(v, step, var, std[:, :], rstd[:, :], var_ready, root_ready)
                    v.wait_ge(wa_done, 1)
                    step(v.tensor_copy(wa[:, :], p_wa[:, 0:H]))

            with ExitStack() as p3:
                JG, SL = 2, 4
                G4 = T // (JG * SL)
                OFF = SL
                m16 = sb("m16", [P, SL, JG, CW], BF16, p3)
                hn = sb("hn", [P, 2, Q, F], F32, p3)
                st = sb("st3", [P, 2, CW], F32, p3)
                zero = sb("zero3", [P, 2, P], BF16, p3)
                e_all = sb("e_all", [P, T, H], F32, p3)
                d_all = sb("d_all", [P, H, T], F32, p3)
                kf = sb("kf", [P, H, T], F32, p3)
                mx = sb("mx", [P, 2, H], F32, p3)
                b76 = sb("b76", [P, 1], F32, p3)
                acc = [ps(f"sacc{k}", [P, CW], p3) for k in range(2)]
                p_e = ps("p_e", [P, 512], p3)
                m_done = [sem(f"d_mask{u}") for u in range(SL)]
                mm_done, chunk_done, zeroed = sem("d_mm_done"), sem("d_chunk_done"), sem("d_zeroed")
                scaled, h1_ready, hi_ready = sem("d_scaled"), sem("d_h1_ready"), sem("d_hi_ready")
                h2_ready, h1_stored, h1_kept = sem("d_h2_ready"), sem("d_h1_stored"), sem("d_h1_kept")
                st_ready, st_stored, st_kept = sem("d_st_ready"), sem("d_st_stored"), sem("d_st_kept")
                e_done, steps, diag_in = sem("d_e_done"), sem("d_steps"), sem("d_diag_in")
                rowmax, allmax = sem("d_rowmax"), sem("d_allmax")
                exp_in, exp_out = sem("d_exp_in"), sem("d_exp_out")
                block = p3.enter_context(nc.Block())

                @block.sync
                def _(sp):
                    sp.sem_inc(h1_kept, 2)
                    sp.sem_inc(st_kept, 2)
                    with sp.Fori(0, NG // 2) as qp:
                        for s in range(2):
                            q = 2 * qp + s
                            sp.wait_ge(h1_ready, q + 1)
                            sp.dma_start(h1_d[:, ds(q * Q, Q), :], hn[:, s, :, :]).then_inc(h1_stored, 16)
                            sp.wait_ge(h1_stored, 16 * q + 16)
                            sp.sem_inc(h1_kept, 1)
                    with nc.allow_non_contiguous_dma(reason="a matrix's diagonal has no run"):
                        diag = bass.AP(tensor=adj_t.tensor, offset=0, ap=[[N + 1, P], [P * (N + 1), T], [1, 1]])
                        sp.dma_start(dn[:, :].unsqueeze(2), diag).then_inc(diag_in, 16)
                    with sp.Fori(0, C // 2) as cp:
                        for s in range(2):
                            c = 2 * cp + s
                            sp.wait_ge(st_ready, 2 + c + 1)
                            sp.dma_start(sup_d[:, ds(c * CW, CW)], st[:, s, :]).then_inc(st_stored, 16)
                            sp.wait_ge(st_stored, 16 * c + 16)
                            sp.sem_inc(st_kept, 1)
                    sp.wait_ge(diag_in, 16)

                @block.gpsimd
                def _(pool):
                    pool.memset(zero[:, :, :], 0.0).then_inc(zeroed, 1)
                    pool.wait_ge(rowmax, 1)
                    pool.partition_all_reduce(mx[:, 1, :], mx[:, 0, :], P,
                                              bass.bass_isa.ReduceOp.max).then_inc(allmax, 1)

                @block.scalar
                def _(act):
                    act.sem_inc(st_ready, 2)

                    def even(c, r):
                        for u in range(0, SL, 2):
                            act.wait_ge(mm_done, (c * G4 + r) * SL + u + 1)
                            act.nop(nofuse=True)
                            act.activation(m16[:, u, :, :], mask[:, ds((r * SL + u) * JG, JG), ds(c * CW, CW)],
                                           ACT.Copy).then_inc(m_done[u], 1)

                    def rest(c, s):
                        if G4 > 1:
                            with act.Fori(1, G4) as r:
                                even(c, r)

                    def drain(c, s):
                        act.wait_ge(chunk_done, c + 1)
                        act.nop(nofuse=True)
                        act.wait_ge(st_kept, 2 + c - 1)
                        act.nop(nofuse=True)
                        act.wait_ge(e_done, 2 + c - 1)
                        act.nop(nofuse=True)
                        act.activation(st[:, s, :], acc[s][:, :], ACT.Copy,
                                       scale=1.0 / SPLIT).then_inc(st_ready, 1)

                    run_chunks(act, lambda c, s: even(c, 0), rest, drain)
                    act.wait_ge(exp_in, 1)
                    act.activation(pw[:, :, :].rearrange("p t h -> p h t"), d_all[:, :, :], ACT.Exp,
                                   bias=b76[:, 0:1], scale=1.0 / 16).then_inc(exp_out, 1)
                    act.wait_ge(exp_in, 2)
                    act.activation(g_all[:, :, :], g_all[:, :, :], ACT.Exp).then_inc(exp_out, 1)

                @block.vector
                def _(v):
                    def norm(q, s):
                        v.wait_ge(h1_kept, 2 + q - 1)
                        for k in range(Q):
                            t = ds(q * Q + k, 1)
                            v.tensor_scalar(hn[:, s, k, :], xs[:, t, :].rearrange("p a f -> p (a f)"),
                                            mean[:, t], rstd[:, t], ALU.subtract, ALU.mult).then_inc(scaled, 1)
                        v.wait_ge(scaled, (q + 1) * Q)
                        v.tensor_scalar(hn[:, s, :, :], hn[:, s, :, :], 0.0, None, ALU.max).then_inc(h1_ready, 1)
                        v.wait_ge(h1_ready, q + 1)
                        v.tensor_scalar(h2[:, ds(q * Q, Q), 0, :], hn[:, s, :, :], SPLIT, None, ALU.mult)\
                            .then_inc(hi_ready, 1)
                        v.wait_ge(hi_ready, q + 1)
                        v.scalar_tensor_tensor(h2[:, ds(q * Q, Q), 1, :], hn[:, s, :, :], SPLIT,
                                               h2[:, ds(q * Q, Q), 0, :], ALU.mult,
                                               ALU.subtract).then_inc(h2_ready, 1)

                    def odd(c, r, u):
                        v.wait_ge(mm_done, (c * G4 + r) * SL + u + 1)
                        v.tensor_copy(m16[:, u, :, :], mask[:, ds((r * SL + u) * JG, JG), ds(c * CW, CW)])\
                            .then_inc(m_done[u], 1)

                    step = Steps(v, steps)
                    step(v.memset(b76[:, :], 76.0))
                    with v.Fori(0, G4) as r:
                        for s in range(2):
                            norm(2 * r + s, s)
                            odd(0, r, 2 * s + 1)
                    with v.Fori(1, C) as c:
                        with v.Fori(0, G4) as r:
                            for u in range(1, SL, 2):
                                odd(c, r, u)
                    v.wait_ge(e_done, 2 + C)
                    step(v.tensor_copy(e_all[:, :, :].rearrange("p t h -> p (t h)"), p_e[:, 0:T * H]))
                    step(v.scalar_tensor_tensor(e_all[:, :, :], e_all[:, :, :], 0.2, e_all[:, :, :],
                                                ALU.mult, ALU.max))
                    v.tensor_reduce(mx[:, 0, :], e_all[:, :, :].rearrange("p t h -> p h t"), AX.X, ALU.max)\
                        .then_inc(rowmax, 1)
                    v.wait_ge(allmax, 1)
                    v.tensor_tensor(d_all[:, :, :], e_all[:, :, :].rearrange("p t h -> p h t"),
                                    mx[:, 1, :].unsqueeze(2).to_broadcast([P, H, T]),
                                    ALU.subtract).then_inc(exp_in, 1)
                    v.wait_ge(exp_in, 1)
                    step(v.tensor_scalar(kf[:, :, :], d_all[:, :, :], LOG2E, ROUND, ALU.mult, ALU.add))
                    step(v.tensor_scalar(kf[:, :, :], kf[:, :, :], ROUND, None, ALU.subtract))
                    step(v.scalar_tensor_tensor(g_all[:, :, :], kf[:, :, :], -LN2_HI, d_all[:, :, :],
                                                ALU.mult, ALU.add))
                    v.scalar_tensor_tensor(g_all[:, :, :], kf[:, :, :], -LN2_LO, g_all[:, :, :],
                                           ALU.mult, ALU.add).then_inc(exp_in, 1)
                    step(v.tensor_scalar(kb[:, :, :], kf[:, :, :], 128.0, 128.0 * 1969 - 262144.0,
                                         ALU.mult, ALU.add))
                    v.wait_ge(exp_out, 2)
                    step(v.tensor_scalar(g_all[:, :, :], g_all[:, :, :], SPLIT, None, ALU.mult))

                @block.tensor
                def _(pe):
                    pe.sem_inc(mm_done, OFF)
                    pe.sem_inc(e_done, 2)
                    pe.wait_ge(zeroed, 1)

                    def sums(c, s, r, opens=False, fresh=False):
                        for u in range(SL):
                            if fresh:
                                pe.wait_ge(h2_ready, 2 * r + u // 2 + 1)
                            pe.wait_ge(m_done[u], c * G4 + r + 1)
                            for jt in range(JG):
                                j = (r * SL + u) * JG + jt
                                for part in range(2):
                                    last = pe.matmul(acc[s][:, :],
                                                     h2[:, ds(j, 1), part, :].rearrange("p a f -> p (a f)"),
                                                     m16[:, u, jt, :],
                                                     start=opens and u == jt == part == 0, stop=False,
                                                     skip_group_check=True)
                            last.then_inc(mm_done, 1)

                    def first(c, s, fresh=False):
                        pe.wait_ge(st_ready, 2 + c - 1)
                        sums(c, s, 0, opens=True, fresh=fresh)

                    def rest(c, s, fresh=False):
                        if G4 > 1:
                            with pe.Fori(1, G4) as r:
                                sums(c, s, r, fresh=fresh)
                        pe.matmul(acc[s][:, 0:P], zero[:, 0, :], zero[:, 1, :], start=False, stop=True,
                                  skip_group_check=True).then_inc(chunk_done, 1)

                    def drain(c, s):
                        pe.wait_ge(st_ready, 2 + c + 1)
                        for it in range(Q):
                            last = pe.matmul(p_e[:, ds((c * Q + it) * H, H)], st[:, s, it * P:(it + 1) * P],
                                             wa[:, :], start=True, stop=True)
                        last.then_inc(e_done, 1)

                    first(0, 0, fresh=True)
                    rest(0, 0, fresh=True)
                    if C > 2:
                        with pe.Fori(0, C // 2 - 1) as cp:
                            for s in range(2):
                                first(2 * cp + s + 1, 1 - s)
                                drain(2 * cp + s, s)
                                rest(2 * cp + s + 1, 1 - s)
                    first(C - 1, 1)
                    drain(C - 2, 0)
                    rest(C - 1, 1)
                    drain(C - 1, 1)

        o0_scope.close()

        with ExitStack() as l1:
            xh = sb("xh", [P, H, T, 2, F1], F16, l1)
            with ExitStack() as p5:
                JG, SL = 2, 4
                G4 = T // (JG * SL)
                OFF = SL
                TH = T * H
                m16 = sb("m16b", [P, SL, JG, CW], BF16, p5)
                zero = sb("zero5", [P, 2, P], BF16, p5)
                hg = sb("hg", [P, 2, Q, F], F32, p5)
                gx = sb("gx", [P, H, Q, F], F32, p5)
                rs = sb("rs", [P, TH], F32, p5)
                rsi = sb("rsi", [P, TH], I32, p5)
                rt = sb("rt", [TH, P], BF16, p5)
                p_r = ps("p_r", [P, 512], p5)
                p_rt = ps("p_rt", [P, 512], p5)
                m_done = [sem(f"f_mask{u}") for u in range(SL)]
                mm_done, zeroed, sums_done = sem("f_mm_done"), sem("f_zeroed"), sem("f_sums_done")
                steps, turned, rows_ready, stored = sem("f_steps"), sem("f_turned"), sem("f_rows_ready"), sem("f_stored")
                scale_ready = sem("f_scale_ready")
                h_in = [sem("f_h_in0"), sem("f_h_in1")]
                gx_ready, hi_ready, lo_ready = sem("f_gx_ready"), sem("f_hi_ready"), sem("f_lo_ready")
                block = p5.enter_context(nc.Block())

                @block.sync
                def _(sp):
                    with sp.Fori(0, NG // 2) as qp:
                        for s in range(2):
                            q = 2 * qp + s
                            sp.wait_ge(lo_ready, 2 * H + (q - 1) * H)
                            sp.dma_start(hg[:, s, :, :], h1_d[:, ds(q * Q, Q), :]).then_inc(h_in[s], 16)
                    sp.wait_ge(rows_ready, 1)
                    sp.dma_start(row_d.rearrange("t h p -> (t h) p"), rt[:, :]).then_inc(stored, 16)
                    sp.wait_ge(stored, 16)

                @block.gpsimd
                def _(pool):
                    pool.memset(zero[:, :, :], 0.0).then_inc(zeroed, 1)
                    with pool.Fori(0, C // 2) as cp:
                        for s in range(2):
                            c = 2 * cp + s
                            pool.wait_ge(h_in[s], 16 * (cp + 1))
                            for k in range(H):
                                pool.wait_ge(lo_ready, (c + 1) * H + k + 1)
                                pool.tensor_tensor(gx[:, k, :, :], hg[:, s, :, :],
                                                   g_all[:, k, ds(c * Q, Q)].unsqueeze(2).to_broadcast([P, Q, F]),
                                                   ALU.mult).then_inc(gx_ready, 1)

                @block.scalar
                def _(act):
                    with act.Fori(0, C) as c:
                        with act.Fori(0, G4) as r:
                            for u in range(0, SL, 2):
                                act.wait_ge(mm_done, (c * G4 + r) * SL + u + 1)
                                act.nop(nofuse=True)
                                act.activation(m16[:, u, :, :],
                                               mask[:, ds((r * SL + u) * JG, JG), ds(c * CW, CW)],
                                               ACT.Copy).then_inc(m_done[u], 1)
                    act.wait_ge(turned, 1)
                    act.activation(rt[:, :], p_rt[0:TH, 0:P], ACT.Copy).then_inc(rows_ready, 1)

                @block.vector
                def _(v):
                    v.sem_inc(lo_ready, 2 * H)
                    with v.Fori(0, C // 2) as cp:
                        for s in range(2):
                            c = 2 * cp + s
                            with v.Fori(0, G4) as r:
                                for u in range(1, SL, 2):
                                    v.wait_ge(mm_done, (c * G4 + r) * SL + u + 1)
                                    v.tensor_copy(m16[:, u, :, :],
                                                  mask[:, ds((r * SL + u) * JG, JG), ds(c * CW, CW)])\
                                        .then_inc(m_done[u], 1)
                            for k in range(H):
                                v.wait_ge(gx_ready, c * H + k + 1)
                                v.tensor_copy(xh[:, k, ds(c * Q, Q), 0, 0:F], gx[:, k, :, :])\
                                    .then_inc(hi_ready, 1)
                            for k in range(H):
                                v.wait_ge(hi_ready, c * H + k + 1)
                                v.tensor_tensor(xh[:, k, ds(c * Q, Q), 1, 0:F], gx[:, k, :, :],
                                                xh[:, k, ds(c * Q, Q), 0, 0:F],
                                                ALU.subtract).then_inc(lo_ready, 1)
                    step = Steps(v, steps)
                    step(v.tensor_copy(xh[:, :, :, 0, F], g_all[:, :, :]))
                    step(v.tensor_tensor(xh[:, :, :, 1, F], g_all[:, :, :], xh[:, :, :, 0, F], ALU.subtract))
                    v.wait_ge(sums_done, 1)
                    step(v.tensor_copy(rs[:, :], p_r[:, 0:TH]))
                    step(v.tensor_scalar(rsi[:, :], rs[:, :].bitcast(I32), 23, None, ALU.logical_shift_right))
                    v.tensor_scalar(rs[:, :], rsi[:, :], -2048.0, 2048.0 * 255, ALU.mult, ALU.add)\
                        .then_inc(scale_ready, 1)

                @block.tensor
                def _(pe):
                    pe.sem_inc(mm_done, OFF)
                    pe.wait_ge(zeroed, 1)
                    pe.matmul(p_r[:, 0:TH], zero[:, 0, :], zero[:, 1, 0:TH], start=True, stop=False,
                              skip_group_check=True)
                    with pe.Fori(0, C) as c:
                        with pe.Fori(0, G4) as r:
                            for u in range(SL):
                                pe.wait_ge(m_done[u], c * G4 + r + 1)
                                for jt in range(JG):
                                    j = (r * SL + u) * JG + jt
                                    for it in range(Q):
                                        last = pe.matmul(p_r[:, ds((c * Q + it) * H, H)],
                                                         m16[:, u, jt, it * P:(it + 1) * P],
                                                         pw[:, ds(j, 1), :].rearrange("p a h -> p (a h)"),
                                                         start=False, stop=False, skip_group_check=True)
                                last.then_inc(mm_done, 1)
                    pe.matmul(p_r[:, 0:TH], zero[:, 0, :], zero[:, 1, 0:TH], start=False, stop=True,
                              skip_group_check=True).then_inc(sums_done, 1)
                    pe.wait_ge(scale_ready, 1)
                    pe.transpose(p_rt[0:TH, 0:P], rs[:, :], ident[:, :]).then_inc(turned, 1)

            with ExitStack() as p6:
                JG = Q
                G2 = T // (2 * JG)
                HF1 = H * F1
                JP = 2
                m16 = sb("m16c", [P, 2, JG, CW], BF16, p6)
                uw = sb("uw", [P, H, JG, CW], BF16, p6)
                nrow = sb("nrow", [P, 2, Q, H, P], BF16, p6)
                att = sb("att", [P, 2, H, F], F32, p6)
                rden = sb("rden6", [P, Q, H], F32, p6)
                zero = sb("zero6", [P, P], F16, p6)
                acc = [ps(f"hacc{k}", [P, Q, 512], p6) for k in range(2)]
                row_in = [sem("g_row_in0"), sem("g_row_in1")]
                stored = [sem("g_stored0"), sem("g_stored1")]
                m_done, ma_done, u_done = sem("g_mask_pool"), sem("g_mask_act"), sem("g_u_done")
                va_done, vd_done = sem("g_weights_act"), sem("g_weights_dve")
                mm_done, chunk_done, att_ready = sem("g_mm_done"), sem("g_chunk_done"), sem("g_att_ready")
                zeroed, steps = sem("g_zeroed"), sem("g_steps")
                OU, OM, OA = 2 * H, H, Q
                block = p6.enter_context(nc.Block())

                @block.sync
                def _(sp):
                    sp.sem_inc(stored[0], 16)
                    sp.sem_inc(stored[1], 16)

                    def rows(c, half):
                        src = row_d[ds(c * Q, Q), :, :].rearrange("t h p -> (t h p)")
                        sp.dma_start(nrow[:, half, :, :, :].rearrange("p t h i -> p (t h i)"),
                                     src.partition_broadcast(P)).then_inc(row_in[half], 16)
                    rows(0, 0)
                    rows(1, 1)

                    def store(c):
                        for it in range(Q):
                            sp.wait_ge(att_ready, OA + c * Q + it + 1)
                            sp.dma_start(att_d[:, ds(c * Q + it, 1), :].rearrange("p a f -> p (a f)"),
                                         att[:, it % 2, :, :].rearrange("p h f -> p (h f)"))\
                                .then_inc(stored[it % 2], 16)

                    if C > 2:
                        with sp.Fori(0, C // 2 - 1) as cp:
                            for half in range(2):
                                store(2 * cp + half)
                                rows(2 * cp + half + 2, half)
                    store(C - 2)
                    store(C - 1)
                    sp.wait_ge(stored[0], 16 + 16 * C * 2)
                    sp.wait_ge(stored[1], 16 + 16 * C * 2)
                    sp.wait_ge(row_in[0], 16 * (C // 2))
                    sp.wait_ge(row_in[1], 16 * (C // 2))

                @block.gpsimd
                def _(pool):
                    pool.memset(zero[:, :], 0.0).then_inc(zeroed, 1)
                    with pool.Fori(0, C) as c:
                        with pool.Fori(0, G2) as r:
                            for u in range(2):
                                n = (c * G2 + r) * 2 + u
                                pool.wait_ge(u_done, OU + (n - 1) * H)
                                pool.tensor_copy(m16[:, u, 0:JP, :],
                                                 mask[:, ds((r * 2 + u) * JG, JP), ds(c * CW, CW)])\
                                    .then_inc(m_done, 1)

                @block.scalar
                def _(act):
                    def widen(c, r, u):
                        n = (c * G2 + r) * 2 + u
                        act.wait_ge(u_done, OU + (n - 1) * H)
                        act.nop(nofuse=True)
                        act.activation(m16[:, u, JP:JG, :],
                                       mask[:, ds((r * 2 + u) * JG + JP, JG - JP), ds(c * CW, CW)],
                                       ACT.Copy).then_inc(ma_done, 1)

                    def weights(c, r, u, k):
                        hk = ((c * G2 + r) * 2 + u) * H + k
                        act.wait_ge(u_done, OU + hk + 1)
                        act.nop(nofuse=True)
                        for jt in range(2):
                            j = (r * 2 + u) * JG + jt
                            act.activation(uw[:, k, jt, :].bitcast(I16), uw[:, k, jt, :], ACT.Relu,
                                           bias=kb[:, k, ds(j, 1)]).then_inc(va_done, 1)

                    def turn(c, r, last):
                        for u in range(2):
                            for k in range(H):
                                weights(c, r, u, k)
                                if k == 0 and u == 0:
                                    widen(c, r, 1)
                                elif k == 0 and not last:
                                    widen(c, r + 1, 0)

                    with act.Fori(0, C) as c:
                        widen(c, 0, 0)
                        if G2 > 1:
                            with act.Fori(0, G2 - 1) as r:
                                turn(c, r, False)
                        turn(c, G2 - 1, True)

                @block.vector
                def _(v):
                    v.sem_inc(u_done, OU)
                    v.sem_inc(att_ready, OA)

                    def unit(c, half, r, u):
                        n = (c * G2 + r) * 2 + u
                        v.wait_ge(m_done, n + 1)
                        v.wait_ge(ma_done, n + 1)
                        for k in range(H):
                            hk = n * H + k
                            v.wait_ge(mm_done, OM + hk - H + 1)
                            v.tensor_tensor(uw[:, k, :, :].rearrange("p j (t i) -> p j t i", i=P),
                                            m16[:, u, :, :].rearrange("p j (t i) -> p j t i", i=P),
                                            nrow[:, half, :, k, :].unsqueeze(1).to_broadcast([P, JG, Q, P]),
                                            ALU.mult).then_inc(u_done, 1)
                            v.wait_ge(u_done, OU + hk + 1)
                            for jt in range(2, JG):
                                j = (r * 2 + u) * JG + jt
                                v.tensor_scalar(uw[:, k, jt, :].bitcast(I16), uw[:, k, jt, :],
                                                kb[:, k, ds(j, 1)], 0.0, ALU.add, ALU.max)\
                                    .then_inc(vd_done, 1)

                    def rest(c, half):
                        if G2 > 1:
                            with v.Fori(1, G2) as r:
                                for u in range(2):
                                    unit(c, half, r, u)

                    def drain(c, half, tiles):
                        a = acc[half][:, :, 0:HF1].rearrange("p i (h f) -> p i h f", f=F1)
                        step = Steps(v, steps, c * 2)
                        if tiles[0] == 0:
                            v.wait_ge(att_ready, OA + c * Q)
                            v.wait_ge(chunk_done, c + 1)
                            step(v.tensor_scalar(rden[:, :, :], a[:, :, :, F], 1e-36, None, ALU.max))
                            step(v.reciprocal(rden[:, :, :], rden[:, :, :]))
                        for it in tiles:
                            v.wait_ge(stored[it % 2], 16 + 16 * (2 * c + it // 2))
                            v.tensor_tensor(att[:, it % 2, :, :], a[:, it, :, 0:F],
                                            rden[:, it, :].unsqueeze(2).to_broadcast([P, H, F]),
                                            ALU.mult).then_inc(att_ready, 1)

                    def first(c, half, turn):
                        v.wait_ge(row_in[half], 16 * (turn + 1))
                        unit(c, half, 0, 0)
                        drain(c - 1, 1 - half, (0, 1))
                        unit(c, half, 0, 1)
                        drain(c - 1, 1 - half, (2, 3))

                    v.wait_ge(row_in[0], 16)
                    unit(0, 0, 0, 0)
                    unit(0, 0, 0, 1)
                    rest(0, 0)
                    if C > 2:
                        with v.Fori(0, C // 2 - 1) as cp:
                            for half in range(2):
                                c = 2 * cp + half + 1
                                first(c, 1 - half, cp + half)
                                rest(c, 1 - half)
                    first(C - 1, 1, C // 2 - 1)
                    rest(C - 1, 1)
                    drain(C - 1, 1, (0, 1, 2, 3))

                @block.tensor
                def _(pe):
                    pe.sem_inc(mm_done, OM)
                    pe.wait_ge(zeroed, 1)
                    with pe.Fori(0, C // 2) as cp:
                        for half in range(2):
                            c = 2 * cp + half
                            pe.wait_ge(att_ready, OA + (c - 1) * Q)
                            for it in range(Q):
                                for k in range(H):
                                    pe.matmul(acc[half][:, it, k * F1:(k + 1) * F1], zero[:, :],
                                              xh[:, 0, 0, 0, :], start=k == 0, stop=False, skip_group_check=True)
                            with pe.Fori(0, G2) as r:
                                for u in range(2):
                                    for k in range(H):
                                        hk = ((c * G2 + r) * 2 + u) * H + k
                                        for jt in range(JG):
                                            j = (r * 2 + u) * JG + jt
                                            if jt < 2:
                                                pe.wait_ge(va_done, 2 * hk + jt + 1)
                                            else:
                                                pe.wait_ge(vd_done, 2 * hk + jt - 1)
                                            for it in range(Q):
                                                for part in range(2):
                                                    last = pe.matmul(
                                                        acc[half][:, it, k * F1:(k + 1) * F1],
                                                        uw[:, k, jt, it * P:(it + 1) * P],
                                                        xh[:, k, ds(j, 1), part, :].rearrange("p a f -> p (a f)"),
                                                        start=False, stop=False, skip_group_check=True)
                                        last.then_inc(mm_done, 1)
                            for it in range(Q):
                                for k in range(H):
                                    last = pe.matmul(acc[half][:, it, k * F1:(k + 1) * F1], zero[:, :],
                                                     xh[:, 0, 0, 0, :], start=False, stop=k == H - 1,
                                                     skip_group_check=True)
                            last.then_inc(chunk_done, 1)

        mask_scope.close()
        with ExitStack() as p7:
            gw = sb("gw", [P, H, F], F32, p7)
            wt = [sb(f"wt{k}", [P, 3 * F], F32, p7) for k in range(4)]
            bias = sb("bias", [P, 2, 4 * F], F32, p7)
            bhh = sb("bhh", [P, 2, 2 * F], F32, p7)
            hg = sb("hg7", [P, 2, Q, F], F32, p7)
            xg = sb("xg7", [P, 2, Q, F], F32, p7)
            ag = sb("ag7", [P, 2, Q, H * F], F32, p7)
            s_t = sb("s_t", [P, 2, CW], F32, p7)
            h_t = sb("h_t", [P, CW], F32, p7)
            a_t = sb("a_t", [P, H, CW], F32, p7)
            n_t = sb("n_t", [P, CW], F32, p7)
            bpart = sb("bpart", [P, 2, 3, 4 * F], BF16, p7)
            brow = sb("brow", [P, 2, 4 * F], BF16, p7)
            ones = sb("ones", [P, P], BF16, p7)
            rz = sb("rz", [P, 2, 2, Q, 2 * F], F32, p7)
            new = sb("new", [P, 2, 2, Q, F], F32, p7)
            cell = sb("cell", [P, 2, Q, F], F32, p7)
            y = sb("y", [P, 2, Q, F], F32, p7)
            p_t = [ps(f"p_t7{k}", [P, CW], p7) for k in range(2)]
            p_s = ps("p_s", [P, CW], p7)
            gates = ps("gates", [P, Q, 4 * F], p7)
            loaded, bias_in = sem("h_loaded"), sem("h_bias_in")
            g_in = [sem("h_in0"), sem("h_in1")]
            turned, copied = sem("h_turned"), sem("h_copied")
            gates_done, gates_read = sem("h_gates_done"), sem("h_gates_read")
            ones_ready, bias_ready = sem("h_ones_ready"), sem("h_bias_ready")
            rz_done, n_done = sem("h_rz_done"), sem("h_n_done")
            steps, y_ready = sem("h_steps"), sem("h_y_ready")
            stored = [sem("h_stored0"), sem("h_stored1")]
            block = p7.enter_context(nc.Block())
            parts = [(e_wih_t, e_bih, e_bhh), (n_wih_t, n_bih, n_bhh)]

            @block.sync
            def _(sp):
                def load(q, s):
                    sp.dma_start(s_t[:, s, :], sup_d[:, ds(q * CW, CW)]).then_inc(g_in[s], 16)
                    for to, of in ((hg, h1_d), (xg, x1_d), (ag, att_d)):
                        sp.dma_start(to[:, s, :, :], of[:, ds(q * Q, Q), :]).then_inc(g_in[s], 16)

                for k, (bi, bh) in enumerate(((e_bih, e_bhh), (n_bih, n_bhh))):
                    sp.dma_start(bias[:, k, 0:3 * F], bi.partition_broadcast(P)).then_inc(bias_in, 16)
                    sp.dma_start(bias[:, k, 3 * F:4 * F], bh[2 * F:3 * F].partition_broadcast(P)).then_inc(bias_in, 16)
                    sp.dma_start(bhh[:, k, :], bh[0:2 * F].partition_broadcast(P)).then_inc(bias_in, 16)
                load(0, 0)
                for k, weight in enumerate((e_wih_t, e_whh_t, n_wih_t, n_whh_t)):
                    sp.dma_start(wt[k][:, :], weight).then_inc(loaded, 16)
                sp.dma_start(gw[:, :, :], gat_w.rearrange("h f g -> f h g")).then_inc(loaded, 16)
                sp.sem_inc(stored[0], 16)
                sp.sem_inc(stored[1], 16)

                def store(q, s):
                    sp.wait_ge(y_ready, 2 + q + 1)
                    sp.dma_start(out_v[:, ds(q * Q, Q), :], y[:, s, :, :]).then_inc(stored[s], 16)

                load(1, 1)
                if NG > 2:
                    with sp.Fori(0, NG // 2 - 1) as qp:
                        for s in range(2):
                            store(2 * qp + s, s)
                            load(2 * qp + s + 2, s)
                store(NG - 2, 0)
                store(NG - 1, 1)
                sp.wait_ge(stored[0], 16 + 16 * (NG // 2))
                sp.wait_ge(stored[1], 16 + 16 * (NG // 2))

            @block.gpsimd
            def _(pool):
                pool.memset(ones[:, :], 1.0).then_inc(ones_ready, 1)

            @block.tensor
            def _(pe):
                def turn(q, n, bank, of):
                    pe.wait_ge(copied, 1 + 5 * q + max(n - 1, 0))
                    for k in range(Q):
                        last = pe.transpose(p_t[bank][:, k * P:(k + 1) * P], of(k), ident[:, :])
                    last.then_inc(turned, 1)

                def cell_gates(x_t, wi, wh, g):
                    for k in range(Q):
                        pe.matmul(gates[:, k, :], ones[:, :], brow[:, g, :], start=True, stop=False,
                                  skip_group_check=True)
                        t, h = x_t[:, k * P:(k + 1) * P], h_t[:, k * P:(k + 1) * P]
                        pe.matmul(gates[:, k, 0:2 * F], t, wi[:, 0:2 * F], start=False, stop=False,
                                  skip_group_check=True)
                        pe.matmul(gates[:, k, 0:2 * F], h, wh[:, 0:2 * F], start=False, stop=False,
                                  skip_group_check=True)
                        pe.matmul(gates[:, k, 2 * F:3 * F], t, wi[:, 2 * F:3 * F], start=False, stop=False,
                                  skip_group_check=True)
                        last = pe.matmul(gates[:, k, 3 * F:4 * F], h, wh[:, 2 * F:3 * F], start=False, stop=True,
                                         skip_group_check=True)
                    last.then_inc(gates_done, 1)

                pe.sem_inc(gates_done, 1)
                pe.wait_ge(loaded, 16 * 5)
                pe.wait_ge(ones_ready, 1)
                pe.wait_ge(bias_ready, 1)
                with pe.Fori(0, NG // 2) as qp:
                    for s in range(2):
                        q = 2 * qp + s
                        pe.wait_ge(g_in[s], 64 * (qp + 1))
                        turn(q, 0, 0, lambda k: hg[:, s, k, :])
                        for h in range(H):
                            turn(q, 1 + h, (1 + h) % 2, lambda k: ag[:, s, k, h * F:(h + 1) * F])
                        pe.wait_ge(copied, 1 + 5 * q + 1)
                        pe.wait_ge(gates_read, 1 + 2 * q)
                        cell_gates(s_t[:, s, :], wt[0], wt[1], 0)
                        pe.wait_ge(copied, 1 + 5 * q + 4)
                        for h in range(H):
                            last = pe.matmul(p_s[:, :], gw[:, h, :], a_t[:, h, :], start=h == 0, stop=h == H - 1)
                        last.then_inc(turned, 1)
                        pe.wait_ge(copied, 1 + 5 * q + 5)
                        pe.wait_ge(gates_read, 1 + 2 * q + 1)
                        cell_gates(n_t[:, :], wt[2], wt[3], 1)

            @block.scalar
            def _(act):
                act.sem_inc(copied, 1)
                with act.Fori(0, NG // 2) as qp:
                    for s in range(2):
                        q = 2 * qp + s
                        def copy(n, to, of, scale=1.0):
                            act.wait_ge(turned, 5 * q + n + 1)
                            act.nop(nofuse=True)
                            act.activation(to, of, ACT.Copy, scale=scale).then_inc(copied, 1)

                        act.wait_ge(gates_done, 1 + 2 * q)
                        act.nop(nofuse=True)
                        copy(0, h_t[:, :], p_t[0][:, :])
                        for h in range(H):
                            copy(1 + h, a_t[:, h, :], p_t[(1 + h) % 2][:, :])
                        act.wait_ge(y_ready, 2 + q - 1)
                        for g in range(2):
                            act.wait_ge(gates_done, 1 + 2 * q + g + 1)
                            act.activation(rz[:, s, g, :, :], gates[:, :, 0:2 * F], ACT.Tanh, scale=0.5)\
                               .then_inc(rz_done, 1)
                            if g == 0:
                                copy(4, n_t[:, :], p_s[:, :], 1.0 / H)
                            act.wait_ge(gates_read, 1 + 2 * q + g + 1)
                            act.activation(new[:, s, g, :, :], new[:, s, g, :, :], ACT.Tanh).then_inc(n_done, 1)

            @block.vector
            def _(v):
                v.sem_inc(y_ready, 2)
                v.sem_inc(gates_read, 1)
                step = Steps(v, steps)
                v.wait_ge(bias_in, 16 * 6)
                step(v.tensor_tensor(bias[:, :, 0:2 * F], bias[:, :, 0:2 * F], bhh[:, :, :], ALU.add))
                for part in range(3):
                    step(v.tensor_copy(bpart[:, :, part, :], bias[:, :, :]))
                    if part < 2:
                        step(v.tensor_tensor(bias[:, :, :], bias[:, :, :], bpart[:, :, part, :], ALU.subtract))
                step(v.tensor_scalar(brow[:, :, :], bpart[:, :, 0, :], ident[:, 0:1], None, ALU.mult))
                step(v.scalar_tensor_tensor(brow[:, :, :], bpart[:, :, 1, :], ident[:, 1:2], brow[:, :, :],
                                            ALU.mult, ALU.add))
                v.scalar_tensor_tensor(brow[:, :, :], bpart[:, :, 2, :], ident[:, 2:3], brow[:, :, :],
                                       ALU.mult, ALU.add).then_inc(bias_ready, 1)
                before, per_group = step.n, 10
                with v.Fori(0, NG // 2) as qp:
                    for s in range(2):
                        q = 2 * qp + s
                        step = Steps(v, steps, before + per_group * q)
                        v.wait_ge(g_in[s], 64 * (qp + 1))
                        v.wait_ge(y_ready, 2 + q)
                        for g in range(2):
                            r = rz[:, s, g, :, 0:F]
                            v.wait_ge(rz_done, 2 * q + g + 1)
                            step(v.scalar_tensor_tensor(new[:, s, g, :, :], r, 1.0, gates[:, :, 3 * F:4 * F],
                                                        ALU.add, ALU.mult))
                            v.scalar_tensor_tensor(new[:, s, g, :, :], new[:, s, g, :, :], 0.5,
                                                   gates[:, :, 2 * F:3 * F], ALU.mult, ALU.add)\
                                .then_inc(gates_read, 1)
                        for g in range(2):
                            z = rz[:, s, g, :, F:2 * F]
                            v.wait_ge(n_done, 2 * q + g + 1)
                            step(v.tensor_tensor(cell[:, g, :, :], hg[:, s, :, :], new[:, s, g, :, :], ALU.subtract))
                            step(v.scalar_tensor_tensor(cell[:, g, :, :], z, 1.0, cell[:, g, :, :],
                                                        ALU.add, ALU.mult))
                            step(v.scalar_tensor_tensor(cell[:, g, :, :], cell[:, g, :, :], 0.5,
                                                        new[:, s, g, :, :], ALU.mult, ALU.add))
                        step(v.tensor_tensor(cell[:, 0, :, :], cell[:, 0, :, :], cell[:, 1, :, :], ALU.add))
                        step(v.tensor_tensor(cell[:, 0, :, :], cell[:, 0, :, :],
                                             dn[:, ds(q * Q, Q)].unsqueeze(2).to_broadcast([P, Q, F]), ALU.mult))
                        v.wait_ge(stored[s], 16 + 16 * qp)
                        v.tensor_tensor(y[:, s, :, :], cell[:, 0, :, :], xg[:, s, :, :], ALU.add)\
                            .then_inc(y_ready, 1)
                        assert step.n == per_group


def kernel(x, adj, L0_gnn_W, L0_gnn_attn_src, L0_gnn_attn_dst, L1_gnn_gat_W, L1_gnn_gat_a,
           L1_gnn_edge_Wih, L1_gnn_edge_Whh, L1_gnn_edge_bih, L1_gnn_edge_bhh,
           L1_gnn_node_Wih, L1_gnn_node_Whh, L1_gnn_node_bih, L1_gnn_node_bhh):
    import numpy as _np
    import concourse.bacc as _bacc
    from concourse import mybir as _mybir
    from concourse.bass_utils import run_bass_kernel_spmd as _run

    t = lambda a: _np.ascontiguousarray(_np.asarray(a).T)
    c = lambda a: _np.ascontiguousarray(_np.asarray(a))
    gw = c(L1_gnn_gat_W)
    arrays = {
        "x": c(x), "adj_t": t(adj), "w0": c(L0_gnn_W), "w0_t": t(L0_gnn_W),
        "att_src": c(L0_gnn_attn_src), "att_dst": c(L0_gnn_attn_dst),
        "gat_w": gw, "gat_w_t": _np.ascontiguousarray(gw.transpose(0, 2, 1)), "gat_a": c(L1_gnn_gat_a),
        "e_wih_t": t(L1_gnn_edge_Wih), "e_whh_t": t(L1_gnn_edge_Whh),
        "e_bih": c(L1_gnn_edge_bih), "e_bhh": c(L1_gnn_edge_bhh),
        "n_wih_t": t(L1_gnn_node_Wih), "n_whh_t": t(L1_gnn_node_Whh),
        "n_bih": c(L1_gnn_node_bih), "n_bhh": c(L1_gnn_node_bhh),
    }
    nc = _bacc.Bacc("TRN2", target_bir_lowering=False, num_devices=1)
    args = {n: nc.dram_tensor(f"in_{n}", a.shape, _mybir.dt.from_np(a.dtype), kind="ExternalInput").ap()
            for n, a in arrays.items()}
    out = nc.dram_tensor("out_x", arrays["x"].shape, _mybir.dt.float32, kind="ExternalOutput").ap()
    graph_layers(nc, out=out, **args)
    r = _run(nc, [{f"in_{n}": a for n, a in arrays.items()}], core_ids=[0])
    return r.results[0]["out_x"]
```
